# Optimizing a Trainium2 kernel written in Bass

```python
import numpy as np
import jax
import jax.numpy as jnp

def _softmax(x, axis=-1):
    return jax.nn.softmax(x, axis=axis)

def _gelu(x):
    return jax.nn.gelu(x, approximate=True)

def _silu(x):
    return jax.nn.silu(x)

def _sigmoid(x):
    return jax.nn.sigmoid(x)

def _layernorm(x, axis=-1, eps=1e-05):
    m = jnp.mean(x, axis=axis, keepdims=True)
    v = jnp.var(x, axis=axis, keepdims=True)
    return (x - m) / jnp.sqrt(v + eps)

def _scatter_add(tgt, idx, src, axis=0):
    return tgt.at[idx].add(src)

def _segment_sum(src, seg, n):
    return jax.ops.segment_sum(src, seg, n)
kernel_name = 'mk_gnn_resnorm_d4_gnn_r32_4c6b42'

def setup_inputs(seed: int=0):
    np.random.seed(seed)
    _w = jnp.asarray

    def _rec_inputs():
        import jax
        import jax.numpy as jnp
        _gk = jax.random.key(seed)
        x = -0.0006008 + 1.001 * jax.random.normal(jax.random.fold_in(_gk, 1), (3125, 256), jnp.float32)
        src = jax.random.randint(jax.random.fold_in(_gk, 2), (50000,), 0, 3125, jnp.int32)
        dst = jax.random.randint(jax.random.fold_in(_gk, 3), (50000,), 0, 3125, jnp.int32)
        _o = jnp.argsort(dst, stable=True)
        src = src[_o]
        dst = dst[_o]
        edge_type_3 = jax.random.randint(jax.random.fold_in(_gk, 14), (50000,), 0, 3, jnp.int32)
        edge_weight = 0.00540447 + 1.00226 * jax.random.normal(jax.random.fold_in(_gk, 15), (50000,), jnp.float32)
        return (x, src, dst, edge_type_3, edge_weight)
    x, src, dst, edge_type_3, edge_weight = _rec_inputs()

    def _L0_gnn_setup():
        import jax, jax.numpy as jnp
        import numpy as np
        N_NODES = 10000
        N_EDGES = 10000
        D_IN = 256
        D_OUT = 256
        MAX_NORM = 0.95

        def _expmap0(u):
            un = jnp.linalg.norm(u, axis=-1, keepdims=True)
            un_c = jnp.maximum(un, 1e-15)
            return jnp.tanh(un_c) * u / un_c
        key = jax.random.key(seed)
        ks = jax.random.split(key, 7)
        x = jax.random.normal(ks[0], (N_NODES, D_IN), dtype=jnp.float32)
        edge_index = jax.random.randint(ks[1], (2, N_EDGES), 0, N_NODES, dtype=jnp.int64)
        W = jax.random.normal(ks[2], (D_OUT, D_IN), dtype=jnp.float32) * (1.0 / np.sqrt(D_IN))
        b = jax.random.normal(ks[3], (D_OUT,), dtype=jnp.float32) * 0.02
        mag_w = jax.random.normal(ks[4], (1, D_IN), dtype=jnp.float32) * 0.02
        mag_b = jax.random.normal(ks[5], (1,), dtype=jnp.float32) * 0.02
        attn_w = jax.random.normal(ks[6], (1, 2 * D_OUT), dtype=jnp.float32) * (1.0 / np.sqrt(2 * D_OUT))
        return {'x': x, 'edge_index': edge_index, 'W': W, 'b': b, 'mag_w': mag_w, 'mag_b': mag_b, 'attn_w': attn_w}
    _L0_gnn_all = _L0_gnn_setup()
    _L0_gnn_in = {k: v for k, v in _L0_gnn_all.items() if k in ('W', 'b', 'mag_w', 'mag_b', 'attn_w')}
    del _L0_gnn_all

    def _L1_gnn_setup():
        import jax, jax.numpy as jnp
        import numpy as np
        H = 4
        DH = 64
        HID = 256
        EPS = 1e-05
        N_NODES = 625
        N_EDGES = 10000
        N_LAYERS = 3

        def _layer_norm(x, g, b):
            mu = jnp.mean(x, axis=-1, keepdims=True)
            var = jnp.mean((x - mu) ** 2, axis=-1, keepdims=True)
            return (x - mu) * jax.lax.rsqrt(var + EPS) * g + b

        def _message_passing(h, src, tgt, et, Wq, bq, Wk, bk, Wv, bv, Ee, Wo, bo, n_nodes):
            Q = (h @ Wq.T + bq).reshape(-1, H, DH)
            K = (h @ Wk.T + bk).reshape(-1, H, DH)
            V = (h @ Wv.T + bv).reshape(-1, H, DH)
            scores = jnp.einsum('ehd,egd->ehg', Q[src], K[tgt]) / jnp.sqrt(jnp.float32(DH))
            attn = jax.nn.softmax(scores, axis=-1)
            msg = jnp.einsum('ehg,egd->ehd', attn, V[tgt]).reshape(-1, HID)
            msg = msg + Ee[et]
            proj = msg @ Wo.T + bo
            return jax.ops.segment_sum(proj, src, num_segments=n_nodes)
        key = jax.random.key(seed)
        ks = jax.random.split(key, 16)

        def w(k, shape, s=0.05):
            return jax.random.normal(k, shape, jnp.float32) * s
        return {'x': jax.random.normal(ks[0], (N_NODES, HID), jnp.float32), 'edges': jax.random.randint(ks[1], (N_EDGES, 2), 0, N_NODES), 'edge_types': jax.random.randint(ks[2], (N_EDGES,), 0, 3), 'Win': w(ks[3], (HID, HID)), 'b_in': jnp.zeros((HID,), jnp.float32), 'Wq': w(ks[4], (N_LAYERS, HID, HID)), 'bq': jnp.zeros((N_LAYERS, HID), jnp.float32), 'Wk': w(ks[5], (N_LAYERS, HID, HID)), 'bk': jnp.zeros((N_LAYERS, HID), jnp.float32), 'Wv': w(ks[6], (N_LAYERS, HID, HID)), 'bv': jnp.zeros((N_LAYERS, HID), jnp.float32), 'Eemb': w(ks[7], (N_LAYERS, 3, HID)), 'Wo': w(ks[8], (N_LAYERS, HID, HID)), 'bo': jnp.zeros((N_LAYERS, HID), jnp.float32), 'ln_g': jnp.ones((N_LAYERS, HID), jnp.float32), 'ln_b': jnp.zeros((N_LAYERS, HID), jnp.float32), 'W1': w(ks[9], (HID, HID)), 'b1': jnp.zeros((HID,), jnp.float32), 'W2': w(ks[10], (HID, HID)), 'b2': jnp.zeros((HID,), jnp.float32)}
    _L1_gnn_all = _L1_gnn_setup()
    _L1_gnn_in = {k: v for k, v in _L1_gnn_all.items() if k in ('Win', 'b_in', 'Wq', 'bq', 'Wk', 'bk', 'Wv', 'bv', 'Eemb', 'Wo', 'bo', 'ln_g', 'ln_b', 'W1', 'b1', 'W2', 'b2')}
    del _L1_gnn_all

    def _L2_gnn_setup():
        import jax, jax.numpy as jnp
        import numpy as np
        N_NODES = 30000
        N_EDGES = 15000
        IN_DIM = 256
        OUT_DIM = 256
        HEADS = 8
        HEAD_DIM = OUT_DIM // HEADS
        NEG_SLOPE = 0.2
        LN_EPS = 1e-05
        key = jax.random.key(seed)
        ks = jax.random.split(key, 8)
        x = jax.random.normal(ks[0], (N_NODES, IN_DIM), dtype=jnp.float32)
        edge_index = jax.random.randint(ks[1], (2, N_EDGES), 0, N_NODES, dtype=jnp.int64)
        glorot = 1.0 / np.sqrt(IN_DIM)
        W = jax.random.normal(ks[2], (IN_DIM, HEADS * HEAD_DIM), dtype=jnp.float32) * glorot
        att_src = jax.random.normal(ks[3], (HEADS, HEAD_DIM), dtype=jnp.float32) * (1.0 / np.sqrt(HEAD_DIM))
        att_dst = jax.random.normal(ks[4], (HEADS, HEAD_DIM), dtype=jnp.float32) * (1.0 / np.sqrt(HEAD_DIM))
        bias = jnp.zeros((OUT_DIM,), dtype=jnp.float32)
        gamma = jnp.ones((OUT_DIM,), dtype=jnp.float32)
        beta = jnp.zeros((OUT_DIM,), dtype=jnp.float32)
        return {'x': x, 'edge_index': edge_index, 'W': W, 'att_src': att_src, 'att_dst': att_dst, 'bias': bias, 'gamma': gamma, 'beta': beta}
    _L2_gnn_all = _L2_gnn_setup()
    _L2_gnn_in = {k: v for k, v in _L2_gnn_all.items() if k in ('W', 'att_src', 'att_dst', 'bias', 'gamma', 'beta')}
    del _L2_gnn_all

    def _L3_gnn_setup():
        import jax, jax.numpy as jnp
        import numpy as np
        from itertools import combinations
        NDIM = 256
        BATCH = 2048

        def _build_mat(rots, idx_i, idx_j, ndim):

            def step(mat, t):
                i, j, theta = t
                c = jnp.cos(theta)
                s = jnp.sin(theta)
                ri = mat[i]
                rj = mat[j]
                mat = mat.at[i].set(c * ri - s * rj)
                mat = mat.at[j].set(s * ri + c * rj)
                return (mat, None)
            mat0 = jnp.eye(ndim, dtype=rots.dtype)
            mat, _ = jax.lax.scan(step, mat0, (idx_i, idx_j, rots))
            return mat.T
        key = jax.random.key(seed)
        k1, k2 = jax.random.split(key)
        pairs = np.array(list(combinations(range(NDIM), 2)), dtype=np.int32)
        return {'x': jax.random.normal(k1, (BATCH, NDIM), dtype=jnp.float32), 'rots': jax.random.normal(k2, (pairs.shape[0],), dtype=jnp.float32), 'idx_i': jnp.asarray(pairs[:, 0]), 'idx_j': jnp.asarray(pairs[:, 1])}
    _L3_gnn_all = _L3_gnn_setup()
    _L3_gnn_in = {k: v for k, v in _L3_gnn_all.items() if k in ()}
    del _L3_gnn_all
    return {'x': x, 'src': src, 'dst': dst, 'edge_type_3': edge_type_3, 'edge_weight': edge_weight, 'L0_gnn_W': _L0_gnn_in['W'], 'L0_gnn_b': _L0_gnn_in['b'], 'L0_gnn_mag_w': _L0_gnn_in['mag_w'], 'L0_gnn_mag_b': _L0_gnn_in['mag_b'], 'L0_gnn_attn_w': _L0_gnn_in['attn_w'], 'L1_gnn_Win': _L1_gnn_in['Win'], 'L1_gnn_b_in': _L1_gnn_in['b_in'], 'L1_gnn_Wq': _L1_gnn_in['Wq'], 'L1_gnn_bq': _L1_gnn_in['bq'], 'L1_gnn_Wk': _L1_gnn_in['Wk'], 'L1_gnn_bk': _L1_gnn_in['bk'], 'L1_gnn_Wv': _L1_gnn_in['Wv'], 'L1_gnn_bv': _L1_gnn_in['bv'], 'L1_gnn_Eemb': _L1_gnn_in['Eemb'], 'L1_gnn_Wo': _L1_gnn_in['Wo'], 'L1_gnn_bo': _L1_gnn_in['bo'], 'L1_gnn_ln_g': _L1_gnn_in['ln_g'], 'L1_gnn_ln_b': _L1_gnn_in['ln_b'], 'L1_gnn_W1': _L1_gnn_in['W1'], 'L1_gnn_b1': _L1_gnn_in['b1'], 'L1_gnn_W2': _L1_gnn_in['W2'], 'L1_gnn_b2': _L1_gnn_in['b2'], 'L2_gnn_W': _L2_gnn_in['W'], 'L2_gnn_att_src': _L2_gnn_in['att_src'], 'L2_gnn_att_dst': _L2_gnn_in['att_dst'], 'L2_gnn_bias': _L2_gnn_in['bias'], 'L2_gnn_gamma': _L2_gnn_in['gamma'], 'L2_gnn_beta': _L2_gnn_in['beta']}

def reference(x, src, dst, edge_type_3, edge_weight, L0_gnn_W, L0_gnn_b, L0_gnn_mag_w, L0_gnn_mag_b, L0_gnn_attn_w, L1_gnn_Win, L1_gnn_b_in, L1_gnn_Wq, L1_gnn_bq, L1_gnn_Wk, L1_gnn_bk, L1_gnn_Wv, L1_gnn_bv, L1_gnn_Eemb, L1_gnn_Wo, L1_gnn_bo, L1_gnn_ln_g, L1_gnn_ln_b, L1_gnn_W1, L1_gnn_b1, L1_gnn_W2, L1_gnn_b2, L2_gnn_W, L2_gnn_att_src, L2_gnn_att_dst, L2_gnn_bias, L2_gnn_gamma, L2_gnn_beta):
    import jax
    import jax.numpy as jnp

    def _L0_gnn_ref(x, edge_index, W, b, mag_w, mag_b, attn_w):
        import jax, jax.numpy as jnp
        import numpy as np
        N_NODES = 10000
        N_EDGES = 10000
        D_IN = 256
        D_OUT = 256
        MAX_NORM = 0.95

        def _expmap0(u):
            un = jnp.linalg.norm(u, axis=-1, keepdims=True)
            un_c = jnp.maximum(un, 1e-15)
            return jnp.tanh(un_c) * u / un_c
        N = x.shape[0]
        F_out = W.shape[0]
        h_raw = x @ W.T + b
        h_dir = h_raw / jnp.maximum(jnp.linalg.norm(h_raw, axis=-1, keepdims=True), 1e-12)
        h_mag = jax.nn.sigmoid(x @ mag_w.T + mag_b) * 1.5
        h = h_dir * h_mag
        src, tgt = (edge_index[0], edge_index[1])
        h_src = h[src]
        h_tgt = h[tgt]
        a_s, a_t = (attn_w[0, :F_out], attn_w[0, F_out:])
        scores = h_src @ a_s + h_tgt @ a_t
        mx = jnp.maximum(jax.ops.segment_max(scores, tgt, num_segments=N), -1000000000.0)
        ex = jnp.exp(scores - mx[tgt])
        se = jax.ops.segment_sum(ex, tgt, num_segments=N)
        attn_weights = ex / (se[tgt] + 1e-10)
        agg = jax.ops.segment_sum(h_src * attn_weights[:, None], tgt, num_segments=N)
        h_combined = h + agg
        h_poincare = _expmap0(h_combined)
        norms = jnp.linalg.norm(h_poincare, axis=1, keepdims=True)
        return jnp.where(norms > MAX_NORM, h_poincare * (MAX_NORM / (norms + 1e-08)), h_poincare)

    def _L1_gnn_ref(x, edges, edge_types, Win, b_in, Wq, bq, Wk, bk, Wv, bv, Eemb, Wo, bo, ln_g, ln_b, W1, b1, W2, b2):
        import jax, jax.numpy as jnp
        import numpy as np
        H = 4
        DH = 64
        HID = 256
        EPS = 1e-05
        N_NODES = 625
        N_EDGES = 10000
        N_LAYERS = 3

        def _layer_norm(x, g, b):
            mu = jnp.mean(x, axis=-1, keepdims=True)
            var = jnp.mean((x - mu) ** 2, axis=-1, keepdims=True)
            return (x - mu) * jax.lax.rsqrt(var + EPS) * g + b

        def _message_passing(h, src, tgt, et, Wq, bq, Wk, bk, Wv, bv, Ee, Wo, bo, n_nodes):
            Q = (h @ Wq.T + bq).reshape(-1, H, DH)
            K = (h @ Wk.T + bk).reshape(-1, H, DH)
            V = (h @ Wv.T + bv).reshape(-1, H, DH)
            scores = jnp.einsum('ehd,egd->ehg', Q[src], K[tgt]) / jnp.sqrt(jnp.float32(DH))
            attn = jax.nn.softmax(scores, axis=-1)
            msg = jnp.einsum('ehg,egd->ehd', attn, V[tgt]).reshape(-1, HID)
            msg = msg + Ee[et]
            proj = msg @ Wo.T + bo
            return jax.ops.segment_sum(proj, src, num_segments=n_nodes)
        n_nodes = x.shape[0]
        src, tgt = (edges[:, 0], edges[:, 1])
        hidden = x @ Win.T + b_in
        for l in range(N_LAYERS):
            m = _message_passing(hidden, src, tgt, edge_types, Wq[l], bq[l], Wk[l], bk[l], Wv[l], bv[l], Eemb[l], Wo[l], bo[l], n_nodes)
            hidden = jax.nn.relu(_layer_norm(hidden + m, ln_g[l], ln_b[l]))
        adjustment = jax.nn.relu(hidden @ W1.T + b1) @ W2.T + b2
        return x + adjustment

    def _L2_gnn_ref(x, edge_index, W, att_src, att_dst, bias, gamma, beta):
        import jax, jax.numpy as jnp
        import numpy as np
        N_NODES = 30000
        N_EDGES = 15000
        IN_DIM = 256
        OUT_DIM = 256
        HEADS = 8
        HEAD_DIM = OUT_DIM // HEADS
        NEG_SLOPE = 0.2
        LN_EPS = 1e-05
        N = x.shape[0]
        h = (x @ W).reshape(N, HEADS, HEAD_DIM)
        loops = jnp.arange(N, dtype=edge_index.dtype)
        ei = jnp.concatenate([edge_index, jnp.stack([loops, loops])], axis=1)
        src, dst = (ei[0], ei[1])
        a_src = jnp.einsum('nhd,hd->nh', h, att_src)
        a_dst = jnp.einsum('nhd,hd->nh', h, att_dst)
        e = a_src[src] + a_dst[dst]
        e = jnp.where(e > 0, e, NEG_SLOPE * e)
        m = jax.ops.segment_max(e, dst, num_segments=N)
        ex = jnp.exp(e - m[dst])
        denom = jax.ops.segment_sum(ex, dst, num_segments=N)
        alpha = ex / denom[dst]
        out = jax.ops.segment_sum(h[src] * alpha[:, :, None], dst, num_segments=N)
        out = out.reshape(N, OUT_DIM) + bias
        mu = jnp.mean(out, axis=-1, keepdims=True)
        var = jnp.var(out, axis=-1, keepdims=True)
        out = (out - mu) * jax.lax.rsqrt(var + LN_EPS)
        return out * gamma + beta

    def _L3_gnn_ref(x, rots, idx_i, idx_j):
        import jax, jax.numpy as jnp
        import numpy as np
        from itertools import combinations
        NDIM = 256
        BATCH = 2048

        def _build_mat(rots, idx_i, idx_j, ndim):

            def step(mat, t):
                i, j, theta = t
                c = jnp.cos(theta)
                s = jnp.sin(theta)
                ri = mat[i]
                rj = mat[j]
                mat = mat.at[i].set(c * ri - s * rj)
                mat = mat.at[j].set(s * ri + c * rj)
                return (mat, None)
            mat0 = jnp.eye(ndim, dtype=rots.dtype)
            mat, _ = jax.lax.scan(step, mat0, (idx_i, idx_j, rots))
            return mat.T
        m = _build_mat(rots, idx_i, idx_j, x.shape[-1])
        return x @ m
    edge_index = jnp.stack([src, dst])
    edge_index_t = jnp.stack([src, dst], axis=1)
    x = _layernorm(x + _L0_gnn_ref(x, edge_index, L0_gnn_W, L0_gnn_b, L0_gnn_mag_w, L0_gnn_mag_b, L0_gnn_attn_w), axis=-1)
    x = _layernorm(x + _L1_gnn_ref(x, edge_index_t, edge_type_3, L1_gnn_Win, L1_gnn_b_in, L1_gnn_Wq, L1_gnn_bq, L1_gnn_Wk, L1_gnn_bk, L1_gnn_Wv, L1_gnn_bv, L1_gnn_Eemb, L1_gnn_Wo, L1_gnn_bo, L1_gnn_ln_g, L1_gnn_ln_b, L1_gnn_W1, L1_gnn_b1, L1_gnn_W2, L1_gnn_b2), axis=-1)
    x = _layernorm(x + _L2_gnn_ref(x, edge_index, L2_gnn_W, L2_gnn_att_src, L2_gnn_att_dst, L2_gnn_bias, L2_gnn_gamma, L2_gnn_beta), axis=-1)
    x = _layernorm(x + _L3_gnn_ref(x, edge_weight, src, dst), axis=-1)
    return x

_drawn_inputs = setup_inputs


def setup_inputs(seed=0):
    import zlib

    import numpy as np

    out = dict(_drawn_inputs(seed))
    spreads = {'L1_gnn_b_in': (0.0, 0.1),
     'L1_gnn_bq': (0.0, 0.293),
     'L1_gnn_bk': (0.0, 0.347),
     'L1_gnn_bv': (0.0, 0.1),
     'L1_gnn_bo': (0.0, 0.1),
     'L1_gnn_ln_g': (1.0, 0.2),
     'L1_gnn_ln_b': (0.0, 0.1),
     'L1_gnn_b1': (0.0, 0.1),
     'L1_gnn_b2': (0.0, 0.1),
     'L2_gnn_bias': (0.0, 0.1),
     'L2_gnn_gamma': (1.0, 0.2),
     'L2_gnn_beta': (0.0, 0.1)}
    factors = {'L0_gnn_b': 8.0, 'L0_gnn_mag_w': 8.0, 'L0_gnn_attn_w': 57.281}
    for name, (base, spread) in spreads.items():
        noise = np.random.default_rng([zlib.crc32(name.encode()), seed]).standard_normal(out[name].shape)
        drawn = base * np.exp(spread * noise) if base else spread * noise
        out[name] = jnp.asarray(drawn.astype(out[name].dtype))
    for name, factor in factors.items():
        out[name] = (out[name] * factor).astype(out[name].dtype)
    return out
```

```python
from contextlib import ExitStack, contextmanager

import concourse.bass as bass
from concourse import mybir

ALU = mybir.AluOpType
ACT = mybir.ActivationFunctionType
AX = mybir.AxisListType
F32 = mybir.dt.float32
BF16 = mybir.dt.bfloat16
I32 = mybir.dt.int32

P = 128
N, D, E = 3125, 256, 50000
NT = -(-N // P)
NP = NT * P
LASTN = N - (NT - 1) * P
RT = 392
ET = RT + NT - 1
BT = 4
EX = ET + 2 * BT
TX = BT + EX
KEYPAD = NP - 1
LO = 64
HI = NP // LO
BLK = 98
SBLK = ET // 4
BIG = 1e38
HEADS1, DH1, TYPES = 4, 64, 3
HEADS2 = 8
LN_EPS = 1e-5
CS = 64
CB = 4
NCB = RT * P // (CS * CB)
TWO_PI = 6.283185307179586
PI2_A, PI2_B = 6.28125, 0.0019353071795864769
ROUND = 12582912.0


@contextmanager
def phase(nc, tag, names, gathers=()):
    with ExitStack() as ctx:
        sems = {n: ctx.enter_context(nc.semaphore(f"{tag}_{n}")) for n in names.split()}
        with nc.Block() as block:
            yield block, sems
        for g in gathers:
            nc.gpsimd.dma_reset(range(g.num, g.num + 1))
        for used in (*sems.values(), *gathers):
            nc.gpsimd.sem_clear(used)


def linker(eng, sem):
    count = [0]

    def link(ins):
        count[0] += 1
        ins.then_inc(sem, 1)
        eng.wait_ge(sem, count[0])
    return link


def constants(nc, K, dram):
    with phase(nc, "const", "iota memset chain load eye last") as (block, s):
        @block.gpsimd
        def _(pool):
            pool.memset(K["ident"][:, :], 0.0).then_inc(s["memset"], 1)
            pool.memset(K["earlier"][:, :], 1.0).then_inc(s["memset"], 1)
            pool.memset(K["ones"][:, :], 1.0).then_inc(s["memset"], 1)
            pool.memset(K["later"][:, :], 1.0).then_inc(s["memset"], 1)
            pool.memset(K["zero"][:, :], 0.0).then_inc(s["memset"], 1)
            pool.memset(K["X"][:, NT - 1, :], 0.0).then_inc(s["last"], 1)
            for raw in (K["raw_src"], K["raw_dst"], K["raw_typ"]):
                pool.memset(raw[:, :], KEYPAD).then_inc(s["last"], 1)
            pool.memset(K["raw_w"][:, :], 0.0).then_inc(s["last"], 1)
            pool.iota(K["i_col"][:, :], pattern=[[0, 1]], base=0, channel_multiplier=1).then_inc(s["iota"], 1)
            pool.iota(K["i_row"][:, :], pattern=[[1, 2 * P]], base=0, channel_multiplier=0).then_inc(s["iota"], 1)
            pool.iota(K["i_tiles"][:, :], pattern=[[1, EX]], base=0, channel_multiplier=0).then_inc(s["iota"], 1)
            pool.wait_ge(s["memset"], 5)
            pool.affine_select(out=K["ident"][:, :], in_=K["ident"][:, :], compare_op=ALU.not_equal, fill=1.0,
                               base=0, pattern=[[-1, P]], channel_multiplier=1).then_inc(s["eye"], 1)
            pool.affine_select(out=K["earlier"][:, :], in_=K["earlier"][:, :], compare_op=ALU.is_gt, fill=0.0,
                               base=0, pattern=[[-1, P]], channel_multiplier=1).then_inc(s["eye"], 1)
            pool.affine_select(out=K["later"][:, :], in_=K["later"][:, :], compare_op=ALU.is_gt, fill=0.0,
                               base=0, pattern=[[1, P]], channel_multiplier=-1).then_inc(s["eye"], 1)

        @block.sync
        def _(sp):
            n = 0
            sp.wait_ge(s["last"], 5)
            sp.dma_start(K["X"][:, 0:NT - 1, :],
                         dram["x"][0:(NT - 1) * P, :].rearrange("(t p) d -> p t d", p=P)).then_inc(s["load"], 16)
            sp.dma_start(K["X"][0:LASTN, NT - 1, :], dram["x"][(NT - 1) * P:N, :]).then_inc(s["load"], 16)
            n += 2
            full = E // RT
            for raw, src in ((K["raw_src"], dram["src"]), (K["raw_dst"], dram["dst"]), (K["raw_typ"], dram["typ"]), (K["raw_w"], dram["w"])):
                sp.dma_start(raw[0:full, :], src[0:full * RT].rearrange("(p j) -> p j", j=RT)).then_inc(s["load"], 16)
                sp.dma_start(raw[full:full + 1, 0:E - full * RT],
                             src[full * RT:E].rearrange("(a j) -> a j", a=1)).then_inc(s["load"], 16)
                n += 2
            sp.wait_ge(s["load"], 16 * n)

        @block.vector
        def _(dve):
            link = linker(dve, s["chain"])
            dve.wait_ge(s["iota"], 3)
            dve.tensor_copy(K["col"][:, :], K["i_col"][:, :]).then_inc(s["chain"], 1)
            dve.tensor_copy(K["row"][:, :], K["i_row"][:, :]).then_inc(s["chain"], 1)
            dve.tensor_copy(K["tiles"][:, :], K["i_tiles"][:, :]).then_inc(s["chain"], 1)
            dve.wait_ge(s["chain"], 3)
            link2 = linker(dve, s["eye"])
            dve.wait_ge(s["eye"], 3)
            c = [3]

            def step(ins):
                c[0] += 1
                ins.then_inc(s["eye"], 1)
                dve.wait_ge(s["eye"], c[0])
            step(dve.tensor_scalar(K["i_a"][:, 0:1], K["i_col"][:, :], 1, None, ALU.logical_shift_right))
            step(dve.tensor_scalar(K["i_a"][:, 1:2], K["i_col"][:, :], 1, None, ALU.bitwise_and))
            step(dve.tensor_copy(K["pair_col"][:, 0:2], K["i_a"][:, 0:2]))
            step(dve.tensor_scalar(K["i_b"][:, :], K["i_row"][:, 0:P], 1, None, ALU.logical_shift_right))
            step(dve.tensor_copy(K["pair_row"][:, :], K["i_b"][:, :]))
            step(dve.tensor_scalar(K["i_b"][:, :], K["i_row"][:, 0:P], 1, None, ALU.bitwise_and))
            step(dve.tensor_copy(K["odd_row"][:, :], K["i_b"][:, :]))
            step(dve.tensor_scalar(K["even_col"][:, :], K["pair_col"][:, 1:2], -1.0, 1.0, ALU.mult, ALU.add))
            step(dve.tensor_scalar(K["same_pair"][:, :], K["pair_row"][:, :], K["pair_col"][:, 0:1], None, ALU.is_equal))
            step(dve.tensor_scalar(K["before_pair"][:, :], K["pair_row"][:, :], K["pair_col"][:, 0:1], K["even_col"][:, 0:1],
                                   ALU.is_gt, ALU.mult))
            step(dve.tensor_scalar(K["col1"][:, :], K["col"][:, :], 1.0, None, ALU.add))
            step(dve.scalar_tensor_tensor(out=K["odd_prev"][:, :], in0=K["row"][:, 0:P], scalar=K["col1"][:, 0:1],
                                          in1=K["odd_row"][:, :], op0=ALU.is_equal, op1=ALU.mult))


def sort_edges(nc, K, tag, raw_key, raw_other, keyrow, hirow, rec, kloc, oth, tid, typ):
    with ExitStack() as ctx:
        def sb(name, shape, dt):
            return ctx.enter_context(nc.sbuf_tensor(f"{tag}_{name}", shape, dt))

        def pb(name, shape, dt=F32):
            return ctx.enter_context(nc.psum_tensor(f"{tag}_{name}", shape, dt))

        keyf = sb("keyf", [P, RT], F32)
        i_t = sb("i_t", [P, RT], I32)
        lof = sb("lof", [P, RT], F32)
        hif = sb("hif", [P, RT], F32)
        rawrec = sb("rawrec", [P, RT, 4], I32)
        padrec = sb("padrec", [P, ET, 4], I32)
        keyT = sb("keyT", [P, 4, P], I32)
        hiT_i = sb("hiT_i", [P, 4, P], I32)
        cnt = sb("cnt", [LO, LO], F32)
        pre = sb("pre", [LO, LO], F32)
        base = sb("base", [LO, LO], F32)
        st = sb("st", [LO, 8], F32)
        sti = sb("sti", [LO, 2], I32)
        tiles_done = sb("tiles_done", [LO, EX], F32)
        tidf = sb("tidf", [1, EX], F32)
        oh_hi = sb("oh_hi", [P, 2, BT, LO], BF16)
        oh_lo = sb("oh_lo", [P, 2, BT, LO], BF16)
        krow = sb("krow", [P, 2, BT, P], I32)
        hrow = sb("hrow", [LO, 2, BT, P], I32)
        hiT = sb("hiT", [LO, 2, BT, P], F32)
        csnap = sb("csnap", [LO, 2 * BT, LO], F32)
        look = sb("look", [P, BT, LO], F32)
        lookr = sb("lookr", [P, 2, BT], F32)
        rank = sb("rank", [P, 2, BT], F32)
        rjunk = sb("rjunk", [P, P], F32)
        place = sb("place", [P, 2, BT], I32)
        recslot = sb("recslot", [P, 2, BT, 4], I32)
        recs = sb("recs", [P, ET, 4], I32)
        ps_t = [pb(f"ps_t{i}", [P, P]) for i in range(4)]
        ps_c = pb("ps_c", [LO, 512])
        ps_l = [pb(f"ps_l{i}", [P, BT, P]) for i in range(2)]

        with phase(nc, tag + "a", "chain turned rows rowst pads padst hot cnt") as (block, s):
            @block.vector
            def _(dve):
                link = linker(dve, s["chain"])
                link(dve.tensor_copy(keyf[:, :], raw_key[:, :]))
                link(dve.tensor_scalar(i_t[:, :], raw_key[:, :], 6, None, ALU.logical_shift_right))
                link(dve.tensor_copy(hif[:, :], i_t[:, :]))
                link(dve.tensor_scalar(i_t[:, :], raw_key[:, :], LO - 1, None, ALU.bitwise_and))
                link(dve.tensor_copy(lof[:, :], i_t[:, :]))
                link(dve.tensor_scalar(i_t[:, :], raw_key[:, :], P - 1, None, ALU.bitwise_and))
                link(dve.tensor_copy(rawrec[:, :, 0], raw_other[:, :]))
                link(dve.tensor_copy(rawrec[:, :, 1], i_t[:, :]))
                link(dve.tensor_copy(rawrec[:, :, 2], K["raw_typ"][:, :]))
                link(dve.tensor_copy(rawrec[:, :, 3], i_t[:, :]))
                link(dve.memset(padrec[:, :, 0], 0))
                link(dve.memset(padrec[:, :, 1], -1))
                link(dve.memset(padrec[:, :, 2], TYPES))
                dve.memset(padrec[:, :, 3], 0).then_inc(s["pads"], 1)
                for g in range(4):
                    dve.wait_ge(s["turned"], g + 1)
                    dve.tensor_copy(keyT[0:BLK, g, :], ps_t[g][0:BLK, :]).then_inc(s["rows"], 1)
                dve.wait_ge(s["rows"], 4)
                dve.tensor_scalar(hiT_i[0:BLK, :, :], keyT[0:BLK, :, :], 6, None,
                                  ALU.logical_shift_right).then_inc(s["rows"], 1)
                with dve.Fori(0, RT // (2 * BT)) as i:
                    for par in range(2):
                        j = i * (2 * BT) + par * BT
                        dve.wait_ge(s["cnt"], i * 2 + par + 1)
                        dve.tensor_tensor(oh_hi[:, par], K["row"][:, 0:LO].unsqueeze(1).broadcast_to([P, BT, LO]),
                                          hif[:, bass.ds(j, BT)].unsqueeze(2).broadcast_to([P, BT, LO]),
                                          ALU.is_equal).then_inc(s["hot"], 1)
                        dve.tensor_tensor(oh_lo[:, par], K["row"][:, 0:LO].unsqueeze(1).broadcast_to([P, BT, LO]),
                                          lof[:, bass.ds(j, BT)].unsqueeze(2).broadcast_to([P, BT, LO]),
                                          ALU.is_equal).then_inc(s["hot"], 1)
                dve.wait_ge(s["cnt"], RT // BT + 2)
                dve.tensor_copy(cnt[:, :], ps_c[:, 0:LO]).then_inc(s["rows"], 1)

            @block.tensor
            def _(pe):
                pe.wait_ge(s["chain"], 1)
                for g in range(4):
                    pe.transpose(ps_t[g][0:BLK, :], keyf[:, g * BLK:(g + 1) * BLK], K["ident"][:, :]).then_inc(s["turned"], 1)
                pe.sem_inc(s["cnt"], 2)
                pe.matmul(ps_c[:, 0:LO], K["zero"][:, 0:LO], K["zero"][:, 0:LO], start=True, stop=False,
                          skip_group_check=True)
                with pe.Fori(0, RT // (2 * BT)) as i:
                    for par in range(2):
                        pe.wait_ge(s["hot"], i * 4 + par * 2 + 2)
                        for u in range(BT):
                            mm = pe.matmul(ps_c[:, 0:LO], oh_hi[:, par, u, :], oh_lo[:, par, u, :],
                                           start=False, stop=True, skip_group_check=True)
                        mm.then_inc(s["cnt"], 1)

            @block.sync
            def _(sp):
                sp.wait_ge(s["rows"], 5)
                for g in range(4):
                    sp.dma_start(keyrow[g * BLK:(g + 1) * BLK, :], keyT[0:BLK, g, :]).then_inc(s["rowst"], 16)
                    sp.dma_start(hirow[g * BLK:(g + 1) * BLK, :], hiT_i[0:BLK, g, :]).then_inc(s["rowst"], 16)
                sp.wait_ge(s["pads"], 1)
                sp.dma_start(rec.rearrange("(p j) c -> p (j c)", p=P),
                             padrec[:, :, :].rearrange("p j c -> p (j c)")).then_inc(s["padst"], 16)
                sp.wait_ge(s["rowst"], 128)
                sp.wait_ge(s["padst"], 16)

        with phase(nc, tag + "b", "chain sums pairs befores dones tids") as (block, s):
            @block.vector
            def _(dve):
                link = linker(dve, s["chain"])
                link(dve.tensor_reduce(st[:, 0:1], cnt[:, :], AX.X, ALU.add))
                link(dve.tensor_tensor_scan(pre[:, :], K["ones"][0:LO, 0:LO], cnt[:, :], 0.0, ALU.mult, ALU.add))
                link(dve.tensor_tensor(base[:, :], pre[:, :], cnt[:, :], ALU.subtract))
                dve.wait_ge(s["pairs"], 1)
                link(dve.tensor_scalar(sti[:, 0:1], ps_c[:, 64:65], float(P - 1), None, ALU.add))
                link(dve.tensor_scalar(sti[:, 1:2], sti[:, 0:1], 7, None, ALU.logical_shift_right))
                link(dve.tensor_copy(st[:, 1:2], sti[:, 1:2]))
                dve.wait_ge(s["befores"], 1)
                link(dve.tensor_copy(st[:, 2:3], ps_c[:, 65:66]))
                link(dve.tensor_scalar(st[:, 3:4], st[:, 2:3], float(P), ps_c[0:LO, 66:67], ALU.mult, ALU.add))
                link(dve.tensor_scalar(base[:, :], base[:, :], st[:, 3:4], None, ALU.add))
                link(dve.tensor_tensor(st[:, 4:5], st[:, 1:2], st[:, 2:3], ALU.add))
                link(dve.tensor_scalar(tiles_done[:, :], K["tiles"][0:LO, :], st[:, 4:5], None, ALU.is_ge))
                dve.wait_ge(s["tids"], 1)
                link(dve.tensor_scalar(tidf[:, :], ps_l[0][0:1, :, :].rearrange("p a b -> p (a b)")[:, 0:EX],
                                       float(NT - 1), None, ALU.min))
                link(dve.memset(tid[:, 0:BT], 0))
                link(dve.tensor_copy(tid[:, BT:TX], tidf[:, :]))

            @block.tensor
            def _(pe):
                pe.wait_ge(s["chain"], 1)
                pe.matmul(ps_c[:, 64:65], K["same_pair"][0:LO, 0:LO], st[:, 0:1], start=True, stop=True).then_inc(s["pairs"], 1)
                pe.wait_ge(s["chain"], 6)
                pe.matmul(ps_c[:, 65:66], K["before_pair"][0:LO, 0:LO], st[:, 1:2], start=True, stop=True,
                          skip_group_check=True)
                pe.matmul(ps_c[:, 66:67], K["odd_prev"][0:LO, 0:LO], st[:, 0:1], start=True, stop=True,
                          skip_group_check=True).then_inc(s["befores"], 1)
                pe.wait_ge(s["chain"], 11)
                pe.matmul(ps_l[0][0:1, :, :].rearrange("p a b -> p (a b)")[:, 0:EX], K["even_col"][0:LO, 0:1],
                          tiles_done[:, :], start=True, stop=True).then_inc(s["tids"], 1)

        with phase(nc, tag + "c", "krow0 krow1 hot snap0 snap rowuse lookd place0 rec q red gate free", K["gathers"]) as (block, s):
            kr = [s["krow0"], s["krow1"]]
            sc = K["gathers"]
            NB = RT // BT

            @block.sync
            def _(sp):
                with sp.Fori(0, NB // 2) as i:
                    for par in range(2):
                        b = i * 2 + par
                        sp.wait_ge(s["rowuse"], b + 1)
                        sp.dma_start(krow[:, par, :, :].rearrange("p a b -> p (a b)"),
                                     keyrow.rearrange("j e -> (j e)")[bass.ds(b * (BT * P), BT * P)].partition_broadcast(P)
                                     ).then_inc(kr[par], 16)
                        sp.dma_start(hrow[:, par, :, :].rearrange("p a b -> p (a b)"),
                                     hirow.rearrange("j e -> (j e)")[bass.ds(b * (BT * P), BT * P)].partition_broadcast(LO)
                                     ).then_inc(kr[par], 16)

            @block.vector
            def _(dve):
                dve.sem_inc(s["rowuse"], 2)
                with dve.Fori(0, NB // 2) as i:
                    for par in range(2):
                        b = i * 2 + par
                        j = i * (2 * BT) + par * BT
                        dve.wait_ge(kr[par], i * 32 + 32)
                        dve.wait_ge(s["snap0"], b * BT + 1)
                        dve.tensor_scalar(hiT[:, par], hrow[:, par], K["col"][0:LO, 0:1], None, ALU.is_equal).then_inc(s["hot"], 1)
                        dve.tensor_tensor(oh_hi[:, par], K["row"][:, 0:LO].unsqueeze(1).broadcast_to([P, BT, LO]),
                                          hif[:, bass.ds(j, BT)].unsqueeze(2).broadcast_to([P, BT, LO]),
                                          ALU.is_equal).then_inc(s["hot"], 1)
                        dve.tensor_tensor(oh_lo[:, par], K["row"][:, 0:LO].unsqueeze(1).broadcast_to([P, BT, LO]),
                                          lof[:, bass.ds(j, BT)].unsqueeze(2).broadcast_to([P, BT, LO]),
                                          ALU.is_equal).then_inc(s["hot"], 1)
                        for u in range(BT):
                            dve.wait_ge(s["q"], b * BT + u + 1)
                            ins = dve.scalar_tensor_tensor(out=rjunk[:, :], in0=krow[:, par, u, :],
                                                           scalar=keyf[:, bass.ds(j + u, 1)], in1=K["earlier"][:, :],
                                                           op0=ALU.is_equal, op1=ALU.mult,
                                                           accum_out=rank[:, par, u:u + 1])
                            ins.then_inc(s["q"], 1)
                        dve.wait_ge(s["q"], b * BT + BT + 1)
                        dve.sem_inc(s["rowuse"], 1)
                        dve.wait_ge(s["snap0"], b * BT + BT + 1)
                        dve.tensor_tensor(look[:, :, :], ps_l[par][:, :, 0:LO], oh_lo[:, par], ALU.mult).then_inc(s["lookd"], 1)
                        dve.wait_ge(s["lookd"], b + 1)
                        dve.tensor_reduce(lookr[:, par], look[:, :, :], AX.X, ALU.add).then_inc(s["red"], 1)
                        dve.wait_ge(s["red"], b + 1)
                        dve.wait_ge(s["free"], b + 1)
                        dve.tensor_tensor(place[:, par], lookr[:, par], rank[:, par], ALU.add).then_inc(s["place0"], 1)

            @block.scalar
            def _(act):
                act.wait_ge(s["snap0"], 1)
                act.activation(csnap[:, 0, :], ps_c[:, 0:LO], ACT.Copy).then_inc(s["snap"], 1)
                act.sem_inc(s["free"], 2)
                with act.Fori(0, NB // 2) as i:
                    for par in range(2):
                        b = i * 2 + par
                        j = i * (2 * BT) + par * BT
                        for u in range(BT):
                            act.wait_ge(s["snap0"], b * BT + u + 2)
                            act.activation(csnap[:, (par * BT + u + 1) % (2 * BT), :], ps_c[:, 0:LO],
                                           ACT.Copy).then_inc(s["snap"], 1)
                        act.wait_ge(s["free"], b + 1)
                        act.activation(recslot[:, par], rawrec[:, bass.ds(j, BT), :], ACT.Copy).then_inc(s["rec"], 1)

            @block.tensor
            def _(pe):
                pe.matmul(ps_c[:, 0:LO], K["ident"][0:LO, 0:LO], base[:, :], start=True, stop=False,
                          skip_group_check=True).then_inc(s["snap0"], 1)
                pe.sem_inc(s["q"], 1)
                with pe.Fori(0, NB // 2) as i:
                    for par in range(2):
                        b = i * 2 + par
                        pe.wait_ge(s["hot"], b * 3 + 3)
                        for u in range(BT):
                            pe.wait_ge(s["snap"], b * BT + u + 1)
                            pe.matmul(ps_l[par][:, u, 0:LO], hiT[:, par, u, :], csnap[:, par * BT + u, :],
                                      start=True, stop=True)
                            pe.matmul(ps_c[:, 0:LO], oh_hi[:, par, u, :], oh_lo[:, par, u, :], start=False,
                                      stop=True, skip_group_check=True).then_inc(s["snap0"], 1)

            @block.gpsimd
            def _(pool):
                with pool.Fori(0, NB // 2) as i:
                    for par in range(2):
                        b = i * 2 + par
                        pool.wait_ge(s["place0"], b + 1)
                        pool.wait_ge(s["rec"], b + 1)
                        pool.sem_inc(s["gate"], 1)
                        for u in range(BT):
                            pool.indirect_dma_start(
                                out=rec, out_offset=bass.IndirectOffsetOnAxis(ap=place[:, par, u:u + 1], axis=0),
                                in_=recslot[:, par, u, :], in_offset=None).then_inc(sc[par], 16)
                    for par in range(2):
                        pool.wait_ge(sc[par], i * (16 * BT) + 16 * BT)
                        pool.sem_inc(s["free"], 1)

        with phase(nc, tag + "d", "load done") as (block, s):
            @block.sync
            def _(sp):
                sp.dma_start(recs[:, :, :], rec.rearrange("(j p) c -> p j c", p=P)).then_inc(s["load"], 16)

            @block.vector
            def _(dve):
                dve.memset(kloc[:, ET:EX], -1.0).then_inc(s["done"], 1)
                dve.memset(oth[:, ET:EX], 0).then_inc(s["done"], 1)
                dve.wait_ge(s["load"], 16)
                dve.tensor_copy(oth[:, 0:ET], recs[:, :, 0]).then_inc(s["done"], 1)
                dve.tensor_copy(kloc[:, 0:ET], recs[:, :, 1]).then_inc(s["done"], 1)
                for c in range(TYPES if typ is not None else 0):
                    dve.tensor_scalar(typ[:, :, c], recs[:, :, 2], float(c), None, ALU.is_equal).then_inc(s["done"], 1)


def segment_marks(nc, K, kloc, brk, last):
    with ExitStack() as ctx:
        kT = ctx.enter_context(nc.sbuf_tensor("mk_kT", [SBLK, 4, P], F32))
        lT = ctx.enter_context(nc.sbuf_tensor("mk_lT", [SBLK, 4, P], F32))
        ps = [ctx.enter_context(nc.psum_tensor(f"mk_ps{i}", [P, P], F32)) for i in range(4)]
        with phase(nc, "mark", "turned marked back chain") as (block, s):
            @block.tensor
            def _(pe):
                for g in range(4):
                    pe.transpose(ps[g][0:SBLK, :], kloc[:, g * SBLK:(g + 1) * SBLK], K["ident"][:, :]).then_inc(s["turned"], 1)
                pe.wait_ge(s["marked"], 1)
                for g in range(4):
                    pe.transpose(ps[g][:, 0:SBLK], lT[:, g, :], K["ident"][0:SBLK, 0:SBLK]).then_inc(s["back"], 1)

            @block.vector
            def _(dve):
                link = linker(dve, s["chain"])
                for g in range(4):
                    dve.wait_ge(s["turned"], g + 1)
                    link(dve.tensor_copy(kT[:, g, :], ps[g][0:SBLK, :]))
                link(dve.memset(brk[:, :, 0:1], 0.0))
                link(dve.tensor_tensor(lT[:, :, 0:P - 1], kT[:, :, 1:P], kT[:, :, 0:P - 1], ALU.not_equal))
                link(dve.tensor_scalar(brk[:, :, 1:P], lT[:, :, 0:P - 1], -BIG, None, ALU.mult))
                link(dve.memset(lT[:, :, P - 1:P], 1.0))
                dve.scalar_tensor_tensor(out=lT[:, :, :], in0=kT[:, :, :], scalar=0.0, in1=lT[:, :, :],
                                         op0=ALU.is_ge, op1=ALU.mult).then_inc(s["marked"], 1)
                for g in range(4):
                    dve.wait_ge(s["back"], g + 1)
                    dve.tensor_copy(last[:, g * SBLK:(g + 1) * SBLK], ps[g][:, 0:SBLK]).then_inc(s["chain"], 1)


def project(nc, tag, K, src, pieces, store=None, extra=None):
    U = 5
    XW = D + (TYPES if extra is not None else 0)
    with ExitStack() as ctx:
        xs = ctx.enter_context(nc.sbuf_tensor(f"{tag}_xs", [P, U, XW], F32))
        xT = ctx.enter_context(nc.sbuf_tensor(f"{tag}_xT", [P, U, 3, P], F32))
        ps_x = [ctx.enter_context(nc.psum_tensor(f"{tag}_psx{i}", [P, 3, P], F32)) for i in range(2)]
        ps_o = [[ctx.enter_context(nc.psum_tensor(f"{tag}_pso{i}_{q}", [P, 512], F32)) for q in range(len(pieces))]
                for i in range(2)]
        names = "xs turn xT mm out free " + " ".join(f"st{u}" for u in range(U))
        with phase(nc, tag, names) as (block, s):
            st = [s["st0"], s["st1"], s["st2"], s["st3"], s["st4"]]

            @block.scalar
            def _(act):
                act.sem_inc(s["turn"], U)
                act.sem_inc(s["out"], 2)
                act.sem_inc(s["free"], U)
                with act.Fori(0, NT // U) as i:
                    for u in range(U):
                        t = i * U + u
                        act.wait_ge(s["turn"], t + 1)
                        act.activation(xs[:, u, :], src[:, bass.ds(t, 1), 0:XW], ACT.Copy).then_inc(s["xs"], 1)
                    for u in range(U):
                        t = i * U + u
                        act.wait_ge(s["mm"], t + 1)
                        if store is not None:
                            act.wait_ge(s["free"], t + 1)
                        for q, (w, bias, C, dst, func) in enumerate(pieces):
                            ins = act.activation(dst(t, u), ps_o[u % 2][q][:, 0:C], func)
                        ins.then_inc(s["out"], 1)

            @block.tensor
            def _(pe):
                with pe.Fori(0, NT // U) as i:
                    for u in range(U):
                        t = i * U + u
                        pe.wait_ge(s["xs"], t + 1)
                        pe.wait_ge(s["xT"], t + 1)
                        for k in range(2):
                            tr = pe.transpose(ps_x[u % 2][:, k, :], xs[:, u, k * P:(k + 1) * P], K["ident"][:, :])
                        if extra is not None:
                            tr = pe.transpose(ps_x[u % 2][0:TYPES, 2, :], xs[:, u, D:XW], K["ident"][:, :])
                        tr.then_inc(s["turn"], 1)
                        pe.wait_ge(s["xT"], t + 2)
                        pe.wait_ge(s["out"], t + (1 if u else 2))
                        for q, (w, bias, C, dst, func) in enumerate(pieces):
                            for k in range(2):
                                mm = pe.matmul(ps_o[u % 2][q][:, 0:C], xT[:, u, k, :], w(k), start=(k == 0),
                                               stop=(k == 1 and bias is None and (q or extra is None)))
                            if bias is not None:
                                mm = pe.matmul(ps_o[u % 2][q][:, 0:C], K["ones"][0:1, :], bias, start=False, stop=True)
                            if q == 0 and extra is not None:
                                mm = pe.matmul(ps_o[u % 2][q][:, 0:C], xT[0:TYPES, u, 2, :], extra, start=False, stop=True)
                        mm.then_inc(s["mm"], 1)

            @block.vector
            def _(dve):
                dve.sem_inc(s["xT"], 1)
                with dve.Fori(0, NT // U) as i:
                    for u in range(U):
                        t = i * U + u
                        dve.wait_ge(s["turn"], t + U + 1)
                        if extra is not None:
                            dve.tensor_copy(xT[0:TYPES, u, 2, :], ps_x[u % 2][0:TYPES, 2, :])
                        dve.tensor_copy(xT[:, u, 0:2, :], ps_x[u % 2][:, 0:2, :]).then_inc(s["xT"], 1)

            if store is not None:
                @block.sync
                def _(sp):
                    with sp.Fori(0, NT // U) as i:
                        for u in range(U):
                            t = i * U + u
                            to, slot = store(t, u)
                            sp.wait_ge(s["out"], t + 3)
                            sp.dma_start(to, slot).then_inc(st[u], 16)
                        for u in range(U):
                            sp.wait_ge(st[u], i * 16 + 16)
                            sp.sem_inc(s["free"], 1)


def one_hot(dve, K, out, kloc, j):
    return dve.tensor_tensor(out, K["row"][:, 0:P].unsqueeze(1).broadcast_to([P, BT, P]),
                             kloc[:, bass.ds(j, BT)].unsqueeze(2).broadcast_to([P, BT, P]), ALU.is_equal)


def tile_ids(eng, tid, j, count=2 * BT):
    return [eng.value_load(tid[0:1, bass.ds(j + v, 1)] if not isinstance(j, int) else tid[0:1, j + v:j + v + 1],
                           min_val=0, max_val=NT - 1) for v in range(count)]


def edge_scores(nc, tag, K, H, kloc, oth, tid, srctab, adst, sall):
    with ExitStack() as ctx:
        def sb(name, shape, dt=F32):
            return ctx.enter_context(nc.sbuf_tensor(f"{tag}_{name}", shape, dt))
        idx = sb("idx", [P, 2, BT], I32)
        ga = sb("ga", [P, 2, BT, H])
        oh = sb("oh", [P, 2, BT, P])
        ohT = sb("ohT", [P, 2, BT, P])
        ps_t = [ctx.enter_context(nc.psum_tensor(f"{tag}_pst{i}", [P, BT, P], F32)) for i in range(2)]
        ps_e = [ctx.enter_context(nc.psum_tensor(f"{tag}_pse{i}", [P, BT, H], F32)) for i in range(2)]
        with phase(nc, tag, "idx hot turn ohT spread s gate", K["gathers"]) as (block, s):
            ga_s = K["gathers"]

            @block.scalar
            def _(act):
                for par in range(2):
                    act.activation(idx[:, par, :], oth[:, par * BT:(par + 1) * BT], ACT.Copy).then_inc(s["idx"], 1)
                with act.Fori(0, ET // (2 * BT)) as i:
                    for par in range(2):
                        b = i * 2 + par
                        j = i * (2 * BT) + par * BT
                        act.wait_ge(s["turn"], b + 1)
                        act.activation(ohT[:, par], ps_t[par][:, :, :], ACT.Copy).then_inc(s["ohT"], 1)
                        act.wait_ge(s["s"], b + 1)
                        act.activation(idx[:, par, :], oth[:, bass.ds(j + 2 * BT, BT)], ACT.Copy).then_inc(s["idx"], 1)

            @block.gpsimd
            def _(pool):
                with pool.Fori(0, ET // (2 * BT)) as i:
                    for par in range(2):
                        pool.wait_ge(s["idx"], i * 2 + par + 1)
                        pool.sem_inc(s["gate"], 1)
                        for u in range(BT):
                            pool.indirect_dma_start(
                                out=ga[:, par, u, :], out_offset=None, in_=srctab,
                                in_offset=bass.IndirectOffsetOnAxis(ap=idx[:, par, u:u + 1], axis=0)
                            ).then_inc(ga_s[par], 16)
                for q in ga_s:
                    pool.wait_ge(q, ET // 2 * 16)

            @block.vector
            def _(dve):
                one_hot(dve, K, oh[:, 0], kloc, 0).then_inc(s["hot"], 1)
                with dve.Fori(0, ET // (2 * BT)) as i:
                    for par in range(2):
                        b = i * 2 + par
                        j = i * (2 * BT) + par * BT
                        dve.wait_ge(s["spread"], b + 1)
                        one_hot(dve, K, oh[:, 1 - par], kloc, j + BT).then_inc(s["hot"], 1)
                        dve.wait_ge(ga_s[par], i * (16 * BT) + 16 * BT)
                        dve.tensor_tensor(sall[:, bass.ds(j, BT), :], ps_e[par][:, :, :], ga[:, par],
                                          ALU.add).then_inc(s["s"], 1)

            @block.tensor
            def _(pe):
                with pe.Fori(0, ET // (2 * BT)) as i:
                    at = tile_ids(pe, tid, i * (2 * BT) + BT)
                    for par in range(2):
                        b = i * 2 + par
                        pe.wait_ge(s["hot"], b + 1)
                        for u in range(BT):
                            tr = pe.transpose(ps_t[par][:, u, :], oh[:, par, u, :], K["ident"][:, :])
                        tr.then_inc(s["turn"], 1)
                        pe.wait_ge(s["ohT"], b + 1)
                        for u in range(BT):
                            mm = pe.matmul(ps_e[par][:, u, :], ohT[:, par, u, :], adst[:, bass.ds(at[par * BT + u], 1), :],
                                           start=True, stop=True)
                        mm.then_inc(s["spread"], 1)


def segment_max(nc, tag, K, H, kloc, tid, brk, last, sall, fl, peak):
    with ExitStack() as ctx:
        def sb(name, shape, dt=F32):
            return ctx.enter_context(nc.sbuf_tensor(f"{tag}_{name}", shape, dt))
        slot = sb("slot", [P, 4, SBLK])
        fT = sb("fT", [SBLK, 4, P])
        oh = sb("oh", [P, 2, BT, P])
        none = sb("none", [P, 2, BT])
        ps_a = [ctx.enter_context(nc.psum_tensor(f"{tag}_psa{i}", [P, P], F32)) for i in range(4)]
        ps_b = [ctx.enter_context(nc.psum_tensor(f"{tag}_psb{i}", [P, 512], F32)) for i in range(4)]
        with phase(nc, tag + "s", "slot turn scan back f") as (block, s):
            @block.scalar
            def _(act):
                act.sem_inc(s["turn"], 4)
                with act.Fori(0, H) as h:
                    for g in range(4):
                        act.wait_ge(s["turn"], h * 4 + g + 1)
                        act.activation(slot[:, g, :], sall[:, g * SBLK:(g + 1) * SBLK, bass.ds(h, 1)],
                                       ACT.Copy).then_inc(s["slot"], 1)

            @block.tensor
            def _(pe):
                with pe.Fori(0, H) as h:
                    for g in range(4):
                        pe.wait_ge(s["slot"], h * 4 + g + 1)
                        pe.wait_ge(s["scan"], h * 4 + g + 1)
                        pe.transpose(ps_a[g][0:SBLK, :], slot[:, g, :], K["ident"][:, :]).then_inc(s["turn"], 1)
                    for g in range(4):
                        pe.wait_ge(s["scan"], h * 4 + g + 5)
                        pe.wait_ge(s["f"], h * 4 + g + 1)
                        pe.transpose(ps_b[g][:, 0:SBLK], fT[:, g, :], K["ident"][0:SBLK, 0:SBLK]).then_inc(s["back"], 1)

            @block.vector
            def _(dve):
                dve.sem_inc(s["scan"], 4)
                dve.sem_inc(s["f"], 4)
                dve.tensor_copy(fl[:, 0:ET, H:H + 1], last[:, :].unsqueeze(2))
                with dve.Fori(0, H) as h:
                    for g in range(4):
                        dve.wait_ge(s["turn"], h * 4 + g + 5)
                        dve.tensor_tensor_scan(fT[:, g, :], brk[:, g, :], ps_a[g][0:SBLK, :], -BIG,
                                               ALU.add, ALU.max).then_inc(s["scan"], 1)
                    for g in range(4):
                        dve.wait_ge(s["back"], h * 4 + g + 1)
                        dve.tensor_tensor(fl[:, g * SBLK:(g + 1) * SBLK, bass.ds(h, 1)],
                                          ps_b[g][:, 0:SBLK].unsqueeze(2),
                                          last[:, g * SBLK:(g + 1) * SBLK].unsqueeze(2), ALU.mult).then_inc(s["f"], 1)

        with phase(nc, tag + "m", "hot mm none peak") as (block, s):
            @block.tensor
            def _(pe):
                with pe.Fori(0, ET // (2 * BT)) as i:
                    for par in range(2):
                        b = i * 2 + par
                        j = i * (2 * BT) + par * BT
                        pe.wait_ge(s["hot"], b + 1)
                        pe.wait_ge(s["peak"], b * BT + BT)
                        for u in range(BT):
                            mm = pe.matmul(ps_b[par][:, u * (H + 1):(u + 1) * (H + 1)], oh[:, par, u, :],
                                           fl[:, bass.ds(j + u, 1), :], start=True, stop=True)
                        mm.then_inc(s["mm"], 1)

            @block.vector
            def _(dve):
                dve.memset(peak[:, :, :], -BIG).then_inc(s["none"], 1)
                dve.sem_inc(s["peak"], 2 * BT)
                one_hot(dve, K, oh[:, 0], kloc, 0).then_inc(s["hot"], 1)
                with dve.Fori(0, ET // (2 * BT)) as i:
                    at = tile_ids(dve, tid, i * (2 * BT) + BT)
                    for par in range(2):
                        b = i * 2 + par
                        j = i * (2 * BT) + par * BT
                        dve.wait_ge(s["mm"], b + 1)
                        got = ps_b[par][:, 0:BT * (H + 1)].rearrange("p (u h) -> p u h", u=BT)
                        dve.tensor_scalar(none[:, par, :], got[:, :, H], BIG, -BIG, ALU.mult, ALU.add).then_inc(s["none"], 1)
                        one_hot(dve, K, oh[:, 1 - par], kloc, j + BT).then_inc(s["hot"], 1)
                        dve.wait_ge(s["none"], b + 2)
                        for u in range(BT):
                            here = peak[:, bass.ds(at[par * BT + u], 1), :]
                            dve.wait_ge(s["peak"], b * BT + u + 2 * BT)
                            dve.scalar_tensor_tensor(out=here, in0=got[:, u:u + 1, 0:H], scalar=none[:, par, u:u + 1],
                                                     in1=here, op0=ALU.add, op1=ALU.max).then_inc(s["peak"], 1)


def edge_sum(nc, tag, K, H, kloc, oth, tid, htab, peak, sall, acc):
    W = D + H
    NB = ET // BT
    with ExitStack() as ctx:
        def sb(name, shape, dt=F32):
            return ctx.enter_context(nc.sbuf_tensor(f"{tag}_{name}", shape, dt))
        idx = sb("idx", [P, 2, BT], I32)
        hg = sb("hg", [P, 2, BT, D])
        val = sb("val", [P, 2, BT, W])
        diff = sb("diff", [P, 2, BT, H])
        oh = sb("oh", [P, 2, BT, P])
        ohT = sb("ohT", [P, 2, BT, P])
        ps_t = ctx.enter_context(nc.psum_tensor(f"{tag}_pst", [P, BT, P], F32))
        ps_e = [ctx.enter_context(nc.psum_tensor(f"{tag}_pse{i}", [P, BT, H], F32)) for i in range(2)]
        ps_g = [ctx.enter_context(nc.psum_tensor(f"{tag}_psg{i}", [P, 512], F32)) for i in range(BT)]
        with phase(nc, tag, "idx hot turn ohT spread diff ex val agg acc gate", K["gathers"]) as (block, s):
            hg_s = K["gathers"]

            @block.scalar
            def _(act):
                for par in range(2):
                    act.activation(idx[:, par, :], oth[:, par * BT:(par + 1) * BT], ACT.Copy).then_inc(s["idx"], 1)
                act.wait_ge(s["turn"], 1)
                act.activation(ohT[:, 0], ps_t[:, :, :], ACT.Copy).then_inc(s["ohT"], 1)
                with act.Fori(0, NB // 2) as i:
                    for par in range(2):
                        b = i * 2 + par
                        j = i * (2 * BT) + par * BT
                        act.wait_ge(s["turn"], b + 2)
                        act.activation(ohT[:, 1 - par], ps_t[:, :, :], ACT.Copy).then_inc(s["ohT"], 1)
                        act.wait_ge(s["diff"], b + 1)
                        act.activation(val[:, par, :, D:W], diff[:, par], ACT.Exp).then_inc(s["ex"], 1)
                        act.wait_ge(s["val"], b + 1)
                        act.activation(idx[:, par, :], oth[:, bass.ds(j + 2 * BT, BT)], ACT.Copy).then_inc(s["idx"], 1)

            @block.gpsimd
            def _(pool):
                with pool.Fori(0, NB // 2) as i:
                    for par in range(2):
                        pool.wait_ge(s["idx"], i * 2 + par + 1)
                        pool.sem_inc(s["gate"], 1)
                        for u in range(BT):
                            pool.indirect_dma_start(
                                out=hg[:, par, u, :], out_offset=None, in_=htab,
                                in_offset=bass.IndirectOffsetOnAxis(ap=idx[:, par, u:u + 1], axis=0)
                            ).then_inc(hg_s[par], 16)
                for q in hg_s:
                    pool.wait_ge(q, ET // 2 * 16)

            @block.vector
            def _(dve):
                dve.memset(acc[:, :, 0:W], 0.0).then_inc(s["acc"], 1)
                one_hot(dve, K, oh[:, 0], kloc, 0).then_inc(s["hot"], 1)

                def take(at, b, u):
                    here = acc[:, bass.ds(at, 1), 0:W]
                    dve.wait_ge(s["acc"], b * BT + u + 1)
                    dve.tensor_tensor(here, ps_g[u][:, 0:W].unsqueeze(1), here, ALU.add).then_inc(s["acc"], 1)

                with dve.Fori(0, NB // 2) as i:
                    at = tile_ids(dve, tid, i * (2 * BT))
                    for par in range(2):
                        b = i * 2 + par
                        j = i * (2 * BT) + par * BT
                        dve.wait_ge(s["spread"], b + 1)
                        dve.tensor_tensor(diff[:, par], sall[:, bass.ds(j, BT), :], ps_e[par][:, :, :],
                                          ALU.subtract).then_inc(s["diff"], 1)
                        dve.wait_ge(s["agg"], b + 1)
                        one_hot(dve, K, oh[:, 1 - par], kloc, j + BT).then_inc(s["hot"], 1)
                        for u in range(BT):
                            take(at[par * BT + u], b, u)
                        dve.wait_ge(s["ex"], b + 1)
                        dve.wait_ge(hg_s[par], i * (16 * BT) + 16 * BT)
                        for u in range(BT):
                            ins = dve.tensor_tensor(
                                val[:, par, u, 0:D].rearrange("p (h d) -> p h d", h=H),
                                hg[:, par, u, :].rearrange("p (h d) -> p h d", h=H),
                                val[:, par, u, D:W].unsqueeze(2).broadcast_to([P, H, D // H]), ALU.mult)
                        ins.then_inc(s["val"], 1)
                at = tile_ids(dve, tid, ET, BT)
                dve.wait_ge(s["agg"], NB + 1)
                for u in range(BT):
                    take(at[u], NB, u)

            @block.tensor
            def _(pe):
                for u in range(BT):
                    mm = pe.matmul(ps_g[u][:, 0:W], K["zero"][:, 0:P], K["zero"][:, 0:W], start=True, stop=True)
                mm.then_inc(s["agg"], 1)
                at0 = tile_ids(pe, tid, BT, BT)

                def spread(at, par, b):
                    pe.wait_ge(s["hot"], b + 1)
                    for u in range(BT):
                        tr = pe.transpose(ps_t[:, u, :], oh[:, par, u, :], K["ident"][:, :])
                    tr.then_inc(s["turn"], 1)
                    pe.wait_ge(s["ohT"], b + 1)
                    for u in range(BT):
                        mm = pe.matmul(ps_e[par][:, u, :], ohT[:, par, u, :], peak[:, bass.ds(at[u], 1), :],
                                       start=True, stop=True)
                    mm.then_inc(s["spread"], 1)

                spread(at0, 0, 0)
                with pe.Fori(0, NB // 2) as i:
                    at = tile_ids(pe, tid, i * (2 * BT) + 2 * BT)
                    for par in range(2):
                        b = i * 2 + par
                        spread(at[par * BT:(par + 1) * BT], 1 - par, b + 1)
                        pe.wait_ge(s["val"], b + 1)
                        pe.wait_ge(s["acc"], b * BT + BT + 1)
                        for u in range(BT):
                            mm = pe.matmul(ps_g[u][:, 0:W], oh[:, par, u, :], val[:, par, u, :], start=True, stop=True)
                        mm.then_inc(s["agg"], 1)


def edge_attention(nc, tag, K, kloc, oth, tid, typ, kvtab, Q, acc):
    W = D + TYPES
    NB = ET // BT
    G = HEADS1
    with ExitStack() as ctx:
        def sb(name, shape, dt=F32):
            return ctx.enter_context(nc.sbuf_tensor(f"{tag}_{name}", shape, dt))
        idx = sb("idx", [P, 2, BT], I32)
        kv = sb("kv", [P, 2, BT, 2 * D])
        prod = sb("prod", [P, BT, G * D])
        mix = sb("mix", [P, BT, G * D])
        sc = sb("sc", [P, BT * G, G])
        top = sb("top", [P, BT * G])
        ex = sb("ex", [P, BT * G, G])
        tot = sb("tot", [P, BT * G])
        att = sb("att", [P, BT * G, G])
        oh = sb("oh", [P, 2, BT, P])
        ohT = sb("ohT", [P, 2, BT, P])
        ps_t = ctx.enter_context(nc.psum_tensor(f"{tag}_pst", [P, BT, P], F32))
        ps_q = [ctx.enter_context(nc.psum_tensor(f"{tag}_psq{i}", [P, 2, D], F32)) for i in range(BT // 2)]
        ps_g = [ctx.enter_context(nc.psum_tensor(f"{tag}_psg{i}", [P, 512], F32)) for i in range(BT)]
        with phase(nc, tag, "idx hot turn ohT spread prod sc top diff ex tot rec att mix agg acc gate",
                   K["gathers"]) as (block, s):
            kv_s = K["gathers"]

            @block.scalar
            def _(act):
                for par in range(2):
                    act.activation(idx[:, par, :], oth[:, par * BT:(par + 1) * BT], ACT.Copy).then_inc(s["idx"], 1)
                act.wait_ge(s["turn"], 1)
                act.activation(ohT[:, 0], ps_t[:, :, :], ACT.Copy).then_inc(s["ohT"], 1)
                with act.Fori(0, NB // 2) as i:
                    for par in range(2):
                        b = i * 2 + par
                        j = i * (2 * BT) + par * BT
                        act.wait_ge(s["turn"], b + 2)
                        act.activation(ohT[:, 1 - par], ps_t[:, :, :], ACT.Copy).then_inc(s["ohT"], 1)
                        act.wait_ge(s["diff"], b + 1)
                        act.activation(ex[:, :, :], sc[:, :, :], ACT.Exp, scale=DH1 ** -0.5).then_inc(s["ex"], 1)
                        act.wait_ge(s["mix"], b + 1)
                        act.activation(idx[:, par, :], oth[:, bass.ds(j + 2 * BT, BT)], ACT.Copy).then_inc(s["idx"], 1)

            @block.gpsimd
            def _(pool):
                with pool.Fori(0, NB // 2) as i:
                    for par in range(2):
                        pool.wait_ge(s["idx"], i * 2 + par + 1)
                        pool.sem_inc(s["gate"], 1)
                        for u in range(BT):
                            pool.indirect_dma_start(
                                out=kv[:, par, u, :], out_offset=None, in_=kvtab,
                                in_offset=bass.IndirectOffsetOnAxis(ap=idx[:, par, u:u + 1], axis=0)
                            ).then_inc(kv_s[par], 16)
                for q in kv_s:
                    pool.wait_ge(q, ET // 2 * 16)

            @block.vector
            def _(dve):
                dve.memset(acc[:, :, 0:W], 0.0).then_inc(s["acc"], 1)
                one_hot(dve, K, oh[:, 0], kloc, 0).then_inc(s["hot"], 1)

                def take(at, b, u):
                    here = acc[:, bass.ds(at, 1), 0:W]
                    dve.wait_ge(s["acc"], b * BT + u + 1)
                    dve.tensor_tensor(here, ps_g[u][:, 0:W].unsqueeze(1), here, ALU.add).then_inc(s["acc"], 1)

                with dve.Fori(0, NB // 2) as i:
                    at = tile_ids(dve, tid, i * (2 * BT))
                    for par in range(2):
                        b = i * 2 + par
                        j = i * (2 * BT) + par * BT
                        dve.wait_ge(s["spread"], b + 1)
                        dve.wait_ge(kv_s[par], i * (16 * BT) + 16 * BT)
                        for u in range(BT):
                            ins = dve.tensor_tensor(
                                prod[:, u, :].rearrange("p (h g d) -> p h g d", h=G, g=G),
                                ps_q[u // 2][:, u % 2, :].rearrange("p (h d) -> p h d", h=G).unsqueeze(2)
                                .broadcast_to([P, G, G, DH1]),
                                kv[:, par, u, 0:D].rearrange("p (g d) -> p g d", g=G).unsqueeze(1)
                                .broadcast_to([P, G, G, DH1]), ALU.mult)
                        ins.then_inc(s["prod"], 1)
                        dve.wait_ge(s["prod"], b + 1)
                        dve.tensor_reduce(sc[:, :, :], prod[:, :, :].rearrange("p u (q d) -> p (u q) d", d=DH1)
                                          .rearrange("p (r g) d -> p r g d", g=G), AX.X, ALU.add).then_inc(s["sc"], 1)
                        dve.wait_ge(s["sc"], b + 1)
                        dve.tensor_reduce(top[:, :], sc[:, :, :], AX.X, ALU.max).then_inc(s["top"], 1)
                        dve.wait_ge(s["top"], b + 1)
                        dve.tensor_tensor(sc[:, :, :], sc[:, :, :], top[:, :].unsqueeze(2).broadcast_to([P, BT * G, G]),
                                          ALU.subtract).then_inc(s["diff"], 1)
                        dve.wait_ge(s["agg"], b + 1)
                        one_hot(dve, K, oh[:, 1 - par], kloc, j + BT).then_inc(s["hot"], 1)
                        for u in range(BT):
                            take(at[par * BT + u], b, u)
                        dve.wait_ge(s["ex"], b + 1)
                        dve.tensor_reduce(tot[:, :], ex[:, :, :], AX.X, ALU.add).then_inc(s["tot"], 1)
                        dve.wait_ge(s["tot"], b + 1)
                        dve.reciprocal(tot[:, :], tot[:, :]).then_inc(s["rec"], 1)
                        dve.wait_ge(s["rec"], b + 1)
                        dve.tensor_tensor(att[:, :, :], ex[:, :, :], tot[:, :].unsqueeze(2).broadcast_to([P, BT * G, G]),
                                          ALU.mult).then_inc(s["att"], 1)
                        dve.wait_ge(s["att"], b + 1)
                        for u in range(BT):
                            ins = dve.tensor_tensor(
                                mix[:, u, :].rearrange("p (g h d) -> p g h d", g=G, h=G),
                                att[:, u * G:(u + 1) * G, :].rearrange("p h g -> p g h").unsqueeze(3)
                                .broadcast_to([P, G, G, DH1]),
                                kv[:, par, u, D:2 * D].rearrange("p (g d) -> p g d", g=G).unsqueeze(2)
                                .broadcast_to([P, G, G, DH1]), ALU.mult)
                        ins.then_inc(s["mix"], 1)
                at = tile_ids(dve, tid, ET, BT)
                dve.wait_ge(s["agg"], NB + 1)
                for u in range(BT):
                    take(at[u], NB, u)

            @block.tensor
            def _(pe):
                for u in range(BT):
                    mm = pe.matmul(ps_g[u][:, 0:W], K["zero"][:, 0:P], K["zero"][:, 0:W], start=True, stop=True)
                mm.then_inc(s["agg"], 1)
                at0 = tile_ids(pe, tid, BT, BT)

                def turn(par, b):
                    pe.wait_ge(s["hot"], b + 1)
                    for u in range(BT):
                        tr = pe.transpose(ps_t[:, u, :], oh[:, par, u, :], K["ident"][:, :])
                    tr.then_inc(s["turn"], 1)

                def spread(at, par, b):
                    pe.wait_ge(s["ohT"], b + 1)
                    for u in range(BT):
                        mm = pe.matmul(ps_q[u // 2][:, u % 2, :], ohT[:, par, u, :], Q[:, bass.ds(at[u], 1), :],
                                       start=True, stop=True)
                    mm.then_inc(s["spread"], 1)

                turn(0, 0)
                spread(at0, 0, 0)
                with pe.Fori(0, NB // 2) as i:
                    at = tile_ids(pe, tid, i * (2 * BT) + 2 * BT)
                    for par in range(2):
                        b = i * 2 + par
                        j = i * (2 * BT) + par * BT
                        turn(1 - par, b + 1)
                        spread(at[par * BT:(par + 1) * BT], 1 - par, b + 1)
                        pe.wait_ge(s["acc"], b * BT + BT + 1)
                        pe.wait_ge(s["mix"], b + 1)
                        for u in range(BT):
                            for g in range(G):
                                pe.matmul(ps_g[u][:, 0:D], oh[:, par, u, :], mix[:, u, g * D:(g + 1) * D],
                                          start=(g == 0), stop=(g == G - 1), skip_group_check=True)
                            mm = pe.matmul(ps_g[u][:, D:W], oh[:, par, u, :], typ[:, bass.ds(j + u, 1), :],
                                           start=False, stop=True, skip_group_check=True)
                        mm.then_inc(s["agg"], 1)


def by_node(v):
    return v.unsqueeze(2).broadcast_to([P, NT, D])


def by_feature(v):
    return v.unsqueeze(1).broadcast_to([P, NT, D])


def normalise(link, dve, act_ready, act_done, y, out, tmp, mean, rstd, at):
    link(dve.tensor_reduce(mean, y, AX.X, ALU.add))
    link(dve.tensor_scalar(mean, mean, 1.0 / D, None, ALU.mult))
    link(dve.tensor_tensor(y, y, by_node(mean), ALU.subtract))
    link(dve.tensor_tensor(tmp, y, y, ALU.mult))
    link(dve.tensor_reduce(rstd, tmp, AX.X, ALU.add))
    dve.tensor_scalar(rstd, rstd, 1.0 / D, LN_EPS, ALU.mult, ALU.add).then_inc(act_ready, 1)
    dve.wait_ge(act_done, at)
    link(dve.reciprocal(rstd, rstd))
    link(dve.tensor_tensor(out, y, by_node(rstd), ALU.mult))


def layer0_nodes(nc, K, H, tmp, maglog, p0, q0, htab, ptab):
    st = K["st"]
    with phase(nc, "l0n", "chain ready act tab") as (block, s):
        @block.vector
        def _(dve):
            link = linker(dve, s["chain"])
            link(dve.tensor_tensor(tmp, H, H, ALU.mult))
            link(dve.tensor_reduce(st[:, 0, :], tmp, AX.X, ALU.add))
            dve.tensor_scalar(st[:, 0, :], st[:, 0, :], 1e-24, None, ALU.max).then_inc(s["ready"], 1)
            link(dve.tensor_tensor(tmp, H, by_feature(K["att0"][:, 0, :]), ALU.mult))
            link(dve.tensor_reduce(st[:, 1, :], tmp, AX.X, ALU.add))
            link(dve.tensor_tensor(tmp, H, by_feature(K["att0"][:, 1, :]), ALU.mult))
            link(dve.tensor_reduce(st[:, 2, :], tmp, AX.X, ALU.add))
            dve.wait_ge(s["act"], 2)
            link(dve.reciprocal(st[:, 0, :], st[:, 0, :]))
            link(dve.scalar_tensor_tensor(out=st[:, 0, :], in0=maglog[:, :, 0], scalar=1.5, in1=st[:, 0, :],
                                          op0=ALU.mult, op1=ALU.mult))
            link(dve.tensor_tensor(p0[:, :, 0], st[:, 1, :], st[:, 0, :], ALU.mult))
            link(dve.tensor_tensor(q0[:, :, 0], st[:, 2, :], st[:, 0, :], ALU.mult))
            dve.tensor_tensor(H, H, by_node(st[:, 0, :]), ALU.mult).then_inc(s["tab"], 1)

        @block.scalar
        def _(act):
            act.wait_ge(s["ready"], 1)
            act.activation(st[:, 0, :], st[:, 0, :], ACT.Sqrt).then_inc(s["act"], 1)
            act.activation(maglog[:, :, 0], maglog[:, :, 0], ACT.Sigmoid).then_inc(s["act"], 1)

        @block.sync
        def _(sp):
            sp.wait_ge(s["tab"], 1)
            sp.dma_start(htab.rearrange("(t p) d -> p t d", p=P), H).then_inc(s["ready"], 16)
            sp.dma_start(ptab.rearrange("(t p) h -> p t h", p=P), p0[:, :, :]).then_inc(s["ready"], 16)
            sp.wait_ge(s["ready"], 33)


def layer0_guard(nc, K, q0, peak):
    with phase(nc, "l0g", "chain") as (block, s):
        @block.vector
        def _(dve):
            dve.tensor_scalar(peak[:, :, :], peak[:, :, :], -1000000000.0, None, ALU.max).then_inc(s["chain"], 1)


def layer0_finish(nc, K, H, acc, tmp):
    st, X = K["st"], K["X"][:, :, :]
    with phase(nc, "l0f", "chain ready act") as (block, s):
        @block.vector
        def _(dve):
            link = linker(dve, s["chain"])
            link(dve.tensor_scalar(st[:, 0, :], acc[:, :, D], 1e-10, None, ALU.add))
            link(dve.reciprocal(st[:, 0, :], st[:, 0, :]))
            link(dve.tensor_tensor(acc[:, :, 0:D], acc[:, :, 0:D], by_node(st[:, 0, :]), ALU.mult))
            link(dve.tensor_tensor(H, H, acc[:, :, 0:D], ALU.add))
            link(dve.tensor_tensor(tmp, H, H, ALU.mult))
            link(dve.tensor_reduce(st[:, 0, :], tmp, AX.X, ALU.add))
            dve.tensor_scalar(st[:, 0, :], st[:, 0, :], 1e-34, None, ALU.max).then_inc(s["ready"], 1)
            dve.wait_ge(s["act"], 1)
            link(dve.tensor_scalar(st[:, 1, :], st[:, 0, :], 1e-15, None, ALU.max))
            dve.reciprocal(st[:, 2, :], st[:, 1, :]).then_inc(s["ready"], 1)
            dve.wait_ge(s["act"], 2)
            dve.wait_ge(s["ready"], 2)
            link(dve.tensor_tensor(st[:, 2, :], st[:, 2, :], st[:, 3, :], ALU.mult))
            link(dve.tensor_tensor(st[:, 3, :], st[:, 2, :], st[:, 0, :], ALU.mult))
            link(dve.tensor_scalar(st[:, 0, :], st[:, 3, :], 1e-8, None, ALU.add))
            link(dve.reciprocal(st[:, 0, :], st[:, 0, :]))
            link(dve.tensor_scalar(st[:, 0, :], st[:, 0, :], 0.95, -1.0, ALU.mult, ALU.add))
            link(dve.scalar_tensor_tensor(out=st[:, 0, :], in0=st[:, 3, :], scalar=0.95, in1=st[:, 0, :],
                                          op0=ALU.is_gt, op1=ALU.mult))
            link(dve.tensor_scalar(st[:, 0, :], st[:, 0, :], 1.0, None, ALU.add))
            link(dve.tensor_tensor(st[:, 0, :], st[:, 0, :], st[:, 2, :], ALU.mult))
            link(dve.tensor_tensor(H, H, by_node(st[:, 0, :]), ALU.mult))
            link(dve.tensor_tensor(X, X, H, ALU.add))
            normalise(link, dve, s["ready"], s["act"], X, X, tmp, st[:, 1, :], st[:, 2, :], 3)

        @block.scalar
        def _(act):
            act.wait_ge(s["ready"], 1)
            act.activation(st[:, 0, :], st[:, 0, :], ACT.Sqrt).then_inc(s["act"], 1)
            act.wait_ge(s["ready"], 2)
            act.activation(st[:, 3, :], st[:, 1, :], ACT.Tanh).then_inc(s["act"], 1)
            act.wait_ge(s["ready"], 3)
            act.activation(st[:, 2, :], st[:, 2, :], ACT.Sqrt).then_inc(s["act"], 1)


def load(nc, tag, pairs):
    with phase(nc, tag, "load") as (block, s):
        @block.sync
        def _(sp):
            for sbuf, dram in pairs:
                sp.dma_start(sbuf, dram).then_inc(s["load"], 16)
            sp.wait_ge(s["load"], 16 * len(pairs))


def dense(nc, tag, K, src, w, b, dst, func):
    with nc.sbuf_tensor(f"{tag}_w", [P, 2, D], F32) as ws, nc.sbuf_tensor(f"{tag}_b", [1, D], F32) as bs:
        load(nc, tag + "l", [(ws[:, :, :], w.rearrange("(k p) n -> p k n", p=P)), (bs[:, :], b.rearrange("(a n) -> a n", a=1))])
        project(nc, tag, K, src, [(lambda k: ws[:, k, :], bs[:, :], D, lambda t, u: dst[:, bass.ds(t, 1), :], func)])


def type_rows(nc, K):
    with nc.psum_tensor("ps_ty", [P, 512], F32) as ps, phase(nc, "ty", "mm cp") as (block, s):
        @block.tensor
        def _(pe):
            for k in range(2):
                pe.matmul(ps[0:TYPES, 0:D], K["eT"][:, k, :], K["wo1"][:, k, :], start=(k == 0), stop=False)
            pe.matmul(ps[0:TYPES, 0:D], K["ones"][0:1, 0:TYPES], K["bo1"][:, :], start=False, stop=True).then_inc(s["mm"], 1)

        @block.vector
        def _(dve):
            dve.wait_ge(s["mm"], 1)
            dve.tensor_copy(K["ty"][:, :], ps[0:TYPES, 0:D]).then_inc(s["cp"], 1)


def layer1_update(nc, K, H, m):
    st = K["st"]
    row = lambda w: by_feature(w[:, :])
    with phase(nc, "l1u", "chain ready act") as (block, s):
        @block.vector
        def _(dve):
            link = linker(dve, s["chain"])
            link(dve.tensor_tensor(H, H, m, ALU.add))
            normalise(link, dve, s["ready"], s["act"], H, H, m, st[:, 1, :], st[:, 2, :], 1)
            link(dve.tensor_tensor(H, H, row(K["lng"]), ALU.mult))
            link(dve.tensor_tensor(H, H, row(K["lnb"]), ALU.add))
            link(dve.tensor_scalar(H, H, 0.0, None, ALU.max))

        @block.scalar
        def _(act):
            act.wait_ge(s["ready"], 1)
            act.activation(st[:, 2, :], st[:, 2, :], ACT.Sqrt).then_inc(s["act"], 1)


def add_and_normalise(nc, tag, K, delta, twice, tmp):
    st, X = K["st"], K["X"][:, :, :]
    with phase(nc, tag, "chain ready act") as (block, s):
        @block.vector
        def _(dve):
            link = linker(dve, s["chain"])
            if twice:
                link(dve.scalar_tensor_tensor(out=X, in0=X, scalar=2.0, in1=delta, op0=ALU.mult, op1=ALU.add))
            else:
                link(dve.tensor_tensor(X, X, delta, ALU.add))
            normalise(link, dve, s["ready"], s["act"], X, X, tmp, st[:, 1, :], st[:, 2, :], 1)

        @block.scalar
        def _(act):
            act.wait_ge(s["ready"], 1)
            act.activation(st[:, 2, :], st[:, 2, :], ACT.Sqrt).then_inc(s["act"], 1)


def by_head(v):
    return v.unsqueeze(3).broadcast_to([P, NT, HEADS2, D // HEADS2])


def heads(v):
    return v.rearrange("p t (h d) -> p t h d", h=HEADS2)


def layer2_nodes(nc, K, H, tmp, asrc, adst, selfs, htab, ptab):
    with phase(nc, "l2n", "chain tab st") as (block, s):
        @block.vector
        def _(dve):
            link = linker(dve, s["chain"])
            for k, a in enumerate((asrc, adst)):
                link(dve.tensor_tensor(tmp, H, by_feature(K["att2"][:, k, :]), ALU.mult))
                link(dve.tensor_reduce(a[:, :, :], heads(tmp), AX.X, ALU.add))
            link(dve.tensor_tensor(selfs[:, :, :], asrc[:, :, :], adst[:, :, :], ALU.add))
            link(dve.scalar_tensor_tensor(out=selfs[:, :, :], in0=selfs[:, :, :], scalar=0.2, in1=selfs[:, :, :],
                                          op0=ALU.mult, op1=ALU.max))

        @block.sync
        def _(sp):
            sp.dma_start(htab.rearrange("(t p) d -> p t d", p=P), H).then_inc(s["tab"], 16)
            sp.wait_ge(s["chain"], 2)
            sp.dma_start(ptab.rearrange("(t p) h -> p t h", p=P), asrc[:, :, :]).then_inc(s["st"], 16)
            sp.wait_ge(s["tab"], 16)
            sp.wait_ge(s["st"], 16)


def layer2_self(nc, K, selfs, peak):
    with phase(nc, "l2s", "chain ex") as (block, s):
        @block.vector
        def _(dve):
            link = linker(dve, s["chain"])
            link(dve.tensor_tensor(peak[:, :, :], peak[:, :, :], selfs[:, :, :], ALU.max))
            dve.tensor_tensor(selfs[:, :, :], selfs[:, :, :], peak[:, :, :], ALU.subtract).then_inc(s["chain"], 1)

        @block.scalar
        def _(act):
            act.wait_ge(s["chain"], 2)
            act.activation(selfs[:, :, :], selfs[:, :, :], ACT.Exp).then_inc(s["ex"], 1)


def layer2_finish(nc, K, H, acc, tmp, selfs, den):
    st, X = K["st"], K["X"][:, :, :]
    out = acc[:, :, 0:D]
    with phase(nc, "l2f", "chain ready act") as (block, s):
        @block.vector
        def _(dve):
            link = linker(dve, s["chain"])
            link(dve.tensor_tensor(heads(H), heads(H), by_head(selfs[:, :, :]), ALU.mult))
            link(dve.tensor_tensor(out, out, H, ALU.add))
            link(dve.tensor_tensor(den[:, :, :], acc[:, :, D:D + HEADS2], selfs[:, :, :], ALU.add))
            link(dve.reciprocal(den[:, :, :], den[:, :, :]))
            link(dve.tensor_tensor(heads(H), heads(out), by_head(den[:, :, :]), ALU.mult))
            link(dve.tensor_tensor(H, H, by_feature(K["bias2"][:, :]), ALU.add))
            normalise(link, dve, s["ready"], s["act"], H, H, tmp, st[:, 1, :], st[:, 2, :], 1)
            link(dve.tensor_tensor(H, H, by_feature(K["gamma2"][:, :]), ALU.mult))
            link(dve.tensor_tensor(H, H, by_feature(K["beta2"][:, :]), ALU.add))
            link(dve.tensor_tensor(X, X, H, ALU.add))
            normalise(link, dve, s["ready"], s["act"], X, X, tmp, st[:, 1, :], st[:, 2, :], 2)

        @block.scalar
        def _(act):
            for k in range(2):
                act.wait_ge(s["ready"], k + 1)
                act.activation(st[:, 2, :], st[:, 2, :], ACT.Sqrt).then_inc(s["act"], 1)


def loop_linker(eng, sem, i, per):
    count = [0]

    def link(ins):
        count[0] += 1
        assert count[0] <= per
        ins.then_inc(sem, 1)
        eng.wait_ge(sem, i * per + count[0])
    return link


def rotation_steps(nc, K, steps, batches):
    full = [P, RT]
    with ExitStack() as ctx:
        def sb(name, shape, dt=F32):
            return ctx.enter_context(nc.sbuf_tensor(f"rs_{name}", shape, dt))
        rec = sb("rec", [P, RT, 4])
        none = sb("none", [P, RT, 4])
        place = sb("place", full)
        act_f = sb("act_f", full)
        a, b, c = sb("a", full), sb("b", full), sb("c", full)
        half_pi = sb("half_pi", [P, 1])
        tot = sb("tot", [P, 2])
        nbi = sb("nbi", [1, 2], I32)
        nbf = sb("nbf", [1, 2])
        placei = sb("placei", [P, 2, BT], I32)
        recslot = sb("recslot", [P, 2, BT, 4])
        ps = ctx.enter_context(nc.psum_tensor("rs_ps", [P, 512], F32))
        with phase(nc, "rsa", "chain sin sins mm pads padst") as (block, s):
            @block.sync
            def _(sp):
                sp.wait_ge(s["pads"], 1)
                sp.dma_start(steps.rearrange("(p j) c -> p (j c)", p=P),
                             none[:, :, :].rearrange("p j c -> p (j c)")).then_inc(s["padst"], 16)
                sp.wait_ge(s["padst"], 16)

            @block.scalar
            def _(act):
                act.wait_ge(s["sin"], 1)
                act.activation(b[:, :], a[:, :], ACT.Sin, scale=0.5).then_inc(s["sins"], 1)
                act.wait_ge(s["sin"], 2)
                act.activation(c[:, :], c[:, :], ACT.Sin, bias=half_pi[:, 0:1], scale=-0.5).then_inc(s["sins"], 1)

            @block.vector
            def _(dve):
                link = linker(dve, s["chain"])
                link(dve.memset(half_pi[:, :], TWO_PI / 4))
                link(dve.memset(none[:, :, 0:2], float(KEYPAD)))
                link(dve.memset(none[:, :, 2:4], 0.0))
                link(dve.tensor_scalar(a[:, :], K["raw_w"][:, :], 1.0 / TWO_PI, ROUND, ALU.mult, ALU.add))
                link(dve.tensor_scalar(a[:, :], a[:, :], ROUND, None, ALU.subtract))
                link(dve.scalar_tensor_tensor(out=b[:, :], in0=a[:, :], scalar=-PI2_A, in1=K["raw_w"][:, :],
                                              op0=ALU.mult, op1=ALU.add))
                link(dve.scalar_tensor_tensor(out=a[:, :], in0=a[:, :], scalar=-PI2_B, in1=b[:, :],
                                              op0=ALU.mult, op1=ALU.add))
                link(dve.tensor_scalar(a[:, :], a[:, :], -TWO_PI / 2, TWO_PI / 2, ALU.max, ALU.min))
                dve.scalar_tensor_tensor(out=c[:, :], in0=a[:, :], scalar=-1.0, in1=a[:, :], op0=ALU.mult,
                                         op1=ALU.max).then_inc(s["sin"], 2)
                link(dve.tensor_copy(rec[:, :, 0], K["raw_src"][:, :]))
                link(dve.tensor_copy(rec[:, :, 1], K["raw_dst"][:, :]))
                dve.memset(tot[:, 1:2], 1.0).then_inc(s["pads"], 1)
                dve.wait_ge(s["sins"], 2)
                link(dve.scalar_tensor_tensor(out=rec[:, :, 2], in0=b[:, :], scalar=-2.0, in1=b[:, :],
                                              op0=ALU.mult, op1=ALU.mult))
                link(dve.scalar_tensor_tensor(out=rec[:, :, 3], in0=b[:, :], scalar=2.0, in1=c[:, :],
                                              op0=ALU.mult, op1=ALU.mult))
                link(dve.tensor_tensor(a[:, :], rec[:, :, 0], rec[:, :, 1], ALU.min))
                link(dve.tensor_scalar(act_f[:, :], a[:, :], float(D), None, ALU.is_lt))
                link(dve.memset(b[:, :], 1.0))
                link(dve.tensor_tensor_scan(place[:, :], b[:, :], act_f[:, :], 0.0, ALU.mult, ALU.add))
                dve.tensor_copy(tot[:, 0:1], place[:, RT - 1:RT]).then_inc(s["pads"], 1)
                dve.wait_ge(s["mm"], 1)
                link(dve.tensor_scalar(place[:, :], place[:, :], ps[:, 0:1], -1.0 - 2.0 * P * RT, ALU.add, ALU.add))
                link(dve.tensor_tensor(place[:, :], place[:, :], act_f[:, :], ALU.mult))
                link(dve.tensor_scalar(place[:, :], place[:, :], 2.0 * P * RT, None, ALU.add))
                link(dve.tensor_scalar(nbi[:, 0:1], ps[0:1, 1:2], float(CS * CB - 1), None, ALU.add))
                link(dve.tensor_scalar(nbi[:, 1:2], nbi[:, 0:1], (CS * CB).bit_length() - 1, None, ALU.logical_shift_right))
                link(dve.tensor_copy(nbf[:, 0:1], nbi[:, 1:2]))
                link(dve.tensor_scalar(nbf[:, 1:2], nbf[:, 0:1], 1.0, None, ALU.max))
                link(dve.tensor_copy(batches[:, :], nbf[:, 1:2]))

            @block.tensor
            def _(pe):
                pe.wait_ge(s["pads"], 2)
                pe.matmul(ps[:, 0:1], K["later"][:, :], tot[:, 0:1], start=True, stop=True, skip_group_check=True)
                pe.matmul(ps[:, 1:2], K["ones"][:, :], tot[:, 0:1], start=True, stop=True,
                          skip_group_check=True).then_inc(s["mm"], 1)

        with phase(nc, "rsb", "rec gate free", K["gathers"]) as (block, s):
            NB = RT // BT
            sc = K["gathers"]

            @block.scalar
            def _(act):
                act.sem_inc(s["free"], 2)
                with act.Fori(0, NB // 2) as i:
                    for par in range(2):
                        j = i * (2 * BT) + par * BT
                        act.wait_ge(s["free"], i * 2 + par + 1)
                        act.activation(recslot[:, par], rec[:, bass.ds(j, BT), :], ACT.Copy)
                        act.activation(placei[:, par], place[:, bass.ds(j, BT)], ACT.Copy).then_inc(s["rec"], 1)

            @block.gpsimd
            def _(pool):
                with pool.Fori(0, NB // 2) as i:
                    for par in range(2):
                        pool.wait_ge(s["rec"], i * 2 + par + 1)
                        pool.sem_inc(s["gate"], 1)
                        for u in range(BT):
                            pool.indirect_dma_start(
                                out=steps, out_offset=bass.IndirectOffsetOnAxis(ap=placei[:, par, u:u + 1], axis=0),
                                in_=recslot[:, par, u, :], in_offset=None, bounds_check=P * RT - 1,
                                oob_is_err=False).then_inc(sc[par], 16)
                    for par in range(2):
                        pool.wait_ge(sc[par], i * (16 * BT) + 16 * BT)
                        pool.sem_inc(s["free"], 1)


def rotation_matrix(nc, K, steps, batches, M):
    with ExitStack() as ctx:
        def sb(name, shape, dt=F32):
            return ctx.enter_context(nc.sbuf_tensor(f"rm_{name}", shape, dt))
        LV = (CS - 1).bit_length()
        ki = sb("ki", [P, 2, P], I32)
        kc = sb("kc", [P, 4], I32)
        kf = sb("kf", [P, P])
        kcf = sb("kcf", [P, 4])
        mask = sb("mask", [P, LV, P])
        maskT = sb("maskT", [P, LV, P])
        rc = sb("rc", [P, 2])
        rec = sb("rec", [P, CB, 4])
        w = sb("w", [P, 6, CB])
        own, oth, alpha, beta = (sb(n, [P, CB]) for n in ("own", "oth", "alpha", "beta"))
        la, lb = sb("la", [P, CB, P]), sb("lb", [P, CB, P])
        Lm, Am = sb("Lm", [P, CB, LV, P]), sb("Am", [P, CB, LV, P])
        Bm, Bx = sb("Bm", [P, CB, D]), sb("Bx", [P, CB, D])
        S = sb("S", [P, CB, D])
        T = sb("T", [P, CB, 2, P])
        V = sb("V", [P, CB, 2, P])
        R = sb("R", [P, CB, 2, P])
        Y = sb("Y", [P, D])
        ps_m = ctx.enter_context(nc.psum_tensor("rm_psm", [P, 2, D], F32))
        ps_r = ctx.enter_context(nc.psum_tensor("rm_psr", [P, CB, P], F32))
        ps_a = ctx.enter_context(nc.psum_tensor("rm_psa", [P, CB, P], F32))
        ps_v = [ctx.enter_context(nc.psum_tensor(f"rm_psv{i}", [P, 2, 2, P], F32)) for i in range(2)]
        ps_w = [ctx.enter_context(nc.psum_tensor(f"rm_psw{i}", [P, 2, 2, P], F32)) for i in range(2)]
        ps_y = ctx.enter_context(nc.psum_tensor("rm_psy", [P, D], F32))

        with phase(nc, "rma", "chain iota") as (block, s):
            @block.gpsimd
            def _(pool):
                pool.iota(ki[:, 0, :], pattern=[[1, P]], base=0, channel_multiplier=0).then_inc(s["iota"], 1)
                pool.iota(kc[:, 0:1], pattern=[[0, 1]], base=0, channel_multiplier=1).then_inc(s["iota"], 1)

            @block.vector
            def _(dve):
                link = linker(dve, s["chain"])
                dve.wait_ge(s["iota"], 2)
                link(dve.tensor_scalar(kc[:, 1:2], kc[:, 0:1], CS - 1, None, ALU.bitwise_and))
                for v in range(LV):
                    link(dve.tensor_scalar(ki[:, 1, :], ki[:, 0, :], CS - 1, v, ALU.bitwise_and, ALU.logical_shift_right))
                    link(dve.tensor_copy(kf[:, :], ki[:, 1, :]))
                    link(dve.tensor_scalar(kc[:, 2:3], kc[:, 1:2], v, None, ALU.logical_shift_right))
                    link(dve.tensor_scalar(kc[:, 3:4], kc[:, 2:3], 1, None, ALU.bitwise_and))
                    link(dve.tensor_copy(kcf[:, 0:2], kc[:, 2:4]))
                    link(dve.tensor_scalar(kcf[:, 2:3], kcf[:, 0:1], -1.0, None, ALU.add))
                    link(dve.tensor_scalar(mask[:, v, :], kf[:, :], kcf[:, 2:3], kcf[:, 1:2], ALU.is_equal, ALU.mult))
                    link(dve.tensor_scalar(kcf[:, 2:3], kcf[:, 0:1], 1.0, None, ALU.add))
                    link(dve.tensor_scalar(kcf[:, 3:4], kcf[:, 1:2], -1.0, 1.0, ALU.mult, ALU.add))
                    link(dve.tensor_scalar(maskT[:, v, :], kf[:, :], kcf[:, 2:3], kcf[:, 3:4], ALU.is_equal, ALU.mult))
                link(dve.tensor_scalar(rc[:, 0:1], K["col"][:, :], float(CS), None, ALU.is_ge))
                link(dve.tensor_scalar(rc[:, 1:2], rc[:, 0:1], 2.0, -1.0, ALU.mult, ALU.add))
                for q in range(2):
                    link(dve.tensor_scalar(Y[:, :], K["row"][:, :], float(-q * P), None, ALU.add))
                    link(dve.tensor_scalar(M[:, q, :], Y[:, :], K["col"][:, 0:1], None, ALU.is_equal))

        with phase(nc, "rmb", "rec free par chain row l turn v vs w tt r rs y ys m ms") as (block, s):
            @block.sync
            def _(sp):
                n = sp.value_load(batches[0:1, 0:1], min_val=1, max_val=NCB)
                with sp.Fori(0, n) as i:
                    sp.wait_ge(s["free"], i + 1)
                    for r in range(2):
                        sp.dma_start(rec[r * CS:(r + 1) * CS, :, :],
                                     steps[bass.ds(i * (CS * CB), CS * CB), :].rearrange("(c k) f -> k c f", k=CS)
                                     ).then_inc(s["rec"], 16)

            @block.vector
            def _(dve):
                n = dve.value_load(batches[0:1, 0:1], min_val=1, max_val=NCB)
                dve.sem_inc(s["free"], 1)
                NPAR = 9
                NCH = NPAR + 4 * CB + 6
                with dve.Fori(0, n) as i:
                    link = loop_linker(dve, s["chain"], i, NCH)
                    dve.wait_ge(s["rec"], i * 32 + 32)
                    I, J, C1, SN = (rec[:, :, q] for q in range(4))
                    link(dve.tensor_tensor(w[:, 0, :], J, I, ALU.subtract))
                    link(dve.scalar_tensor_tensor(out=w[:, 1, :], in0=w[:, 0, :], scalar=rc[:, 0:1], in1=I,
                                                  op0=ALU.mult, op1=ALU.add))
                    link(dve.scalar_tensor_tensor(out=w[:, 2, :], in0=w[:, 0, :], scalar=rc[:, 0:1], in1=J,
                                                  op0=ALU.mult, op1=ALU.subtract))
                    link(dve.tensor_scalar(oth[:, :], w[:, 2, :], -1.0, float(D - 1), ALU.mult, ALU.min))
                    link(dve.tensor_scalar(own[:, :], w[:, 1, :], float(D - 1), None, ALU.min))
                    link(dve.tensor_scalar(w[:, 3, :], w[:, 0, :], 0.0, rc[:, 0:1], ALU.not_equal, ALU.max))
                    link(dve.scalar_tensor_tensor(out=w[:, 4, :], in0=w[:, 1, :], scalar=float(D), in1=w[:, 3, :],
                                                  op0=ALU.is_lt, op1=ALU.mult))
                    link(dve.tensor_tensor(alpha[:, :], w[:, 4, :], C1, ALU.mult))
                    link(dve.scalar_tensor_tensor(out=beta[:, :], in0=SN, scalar=rc[:, 1:2], in1=w[:, 4, :],
                                                  op0=ALU.mult, op1=ALU.mult))
                    dve.sem_inc(s["free"], 1)
                    dve.sem_inc(s["par"], 1)
                    for c in range(CB):
                        link(dve.tensor_scalar(Bm[:, c, :], K["row"][:, :], own[:, c:c + 1], alpha[:, c:c + 1],
                                               ALU.is_equal, ALU.mult))
                        link(dve.tensor_scalar(Bx[:, c, :], K["row"][:, :], oth[:, c:c + 1], beta[:, c:c + 1],
                                               ALU.is_equal, ALU.mult))
                    link(dve.tensor_tensor(Bm[:, :, :], Bm[:, :, :], Bx[:, :, :], ALU.add))
                    dve.wait_ge(s["row"], i + 1)
                    link(dve.tensor_tensor(S[:, :, :], K["row"][:, :].unsqueeze(1).broadcast_to([P, CB, D]),
                                           own[:, :].unsqueeze(2).broadcast_to([P, CB, D]), ALU.is_equal))
                    for c in range(CB):
                        link(dve.tensor_scalar(la[:, c, :], ps_r[:, c, :], own[:, c:c + 1], alpha[:, c:c + 1],
                                               ALU.is_equal, ALU.mult))
                        link(dve.tensor_scalar(lb[:, c, :], ps_r[:, c, :], oth[:, c:c + 1], beta[:, c:c + 1],
                                               ALU.is_equal, ALU.mult))
                    link(dve.tensor_tensor(la[:, :, :], la[:, :, :], lb[:, :, :], ALU.add))
                    dve.sem_inc(s["l"], 1)
                    for c in range(CB):
                        ins = dve.tensor_tensor(Lm[:, c], la[:, c, :].unsqueeze(1).broadcast_to([P, LV, P]),
                                                mask[:, :, :], ALU.mult)
                    link(ins)
                    dve.wait_ge(s["turn"], i + 1)
                    for c in range(CB):
                        ins = dve.tensor_tensor(Am[:, c], ps_a[:, c, :].unsqueeze(1).broadcast_to([P, LV, P]),
                                                maskT[:, :, :], ALU.mult)
                    link(ins)
                    eye = K["ident"][:, :].unsqueeze(1).broadcast_to([P, CB, P])
                    link(dve.tensor_tensor(T[:, :, 0, :], Lm[:, :, 0, :], eye, ALU.add))
                    dve.tensor_tensor(T[:, :, 1, :], Am[:, :, 0, :], eye, ALU.add).then_inc(s["tt"], 1)
                    for v in range(1, LV):
                        dve.wait_ge(s["w"], i * (LV - 1) + v)
                        dve.wait_ge(s["tt"], i * (1 + 2 * (LV - 1)) + 1 + 2 * (v - 1))
                        for q in range(2):
                            dve.tensor_tensor(T[:, 2 * q:2 * q + 2], ps_w[q][:, :, :, :], T[:, 2 * q:2 * q + 2],
                                              ALU.add).then_inc(s["tt"], 1)
                    for c in range(CB):
                        dve.wait_ge(s["y"], i * CB + c + 1)
                        dve.tensor_copy(Y[:, :], ps_y[:, :]).then_inc(s["ys"], 1)

            @block.scalar
            def _(act):
                n = act.value_load(batches[0:1, 0:1], min_val=1, max_val=NCB)
                with act.Fori(0, n) as i:
                    for v in range(1, LV):
                        act.wait_ge(s["v"], i * (LV - 1) + v)
                        for q in range(2):
                            ins = act.activation(V[:, 2 * q:2 * q + 2], ps_v[q][:, :, :, :], ACT.Copy)
                        ins.then_inc(s["vs"], 1)
                    act.wait_ge(s["r"], i + 1)
                    for q in range(2):
                        ins = act.activation(R[:, 2 * q:2 * q + 2], ps_v[q][:, :, :, :], ACT.Copy)
                    ins.then_inc(s["rs"], 1)
                    for c in range(CB):
                        act.wait_ge(s["m"], i * CB + c + 1)
                        act.activation(M[:, :, :], ps_m[:, :, :], ACT.Copy).then_inc(s["ms"], 1)

            @block.tensor
            def _(pe):
                n = pe.value_load(batches[0:1, 0:1], min_val=1, max_val=NCB)
                both = M[:, :, :].rearrange("p q n -> p (q n)")
                pe.matmul(ps_m[:, :, :].rearrange("p q n -> p (q n)"), K["ident"][:, :], both, start=True, stop=True,
                          skip_group_check=True)
                NTT = 1 + 2 * (LV - 1)
                with pe.Fori(0, n) as i:
                    pe.wait_ge(s["par"], i + 1)
                    for c in range(CB):
                        mm = pe.matmul(ps_r[:, c, :], own[:, c:c + 1].broadcast_to([P, P]), K["ident"][:, :],
                                       start=True, stop=True, skip_group_check=True)
                    mm.then_inc(s["row"], 1)
                    pe.wait_ge(s["l"], i + 1)
                    for c in range(CB):
                        tr = pe.transpose(ps_a[:, c, :], la[:, c, :], K["ident"][:, :])
                    tr.then_inc(s["turn"], 1)
                    for v in range(1, LV):
                        pe.wait_ge(s["tt"], i * NTT + 1 + 2 * (v - 1))
                        for c in range(CB):
                            pe.matmul(ps_v[c // 2][:, c % 2, 0, :], Am[:, c, v, :], T[:, c, 0, :], start=True, stop=True,
                                      skip_group_check=True)
                            mm = pe.matmul(ps_v[c // 2][:, c % 2, 1, :], Lm[:, c, v, :], T[:, c, 1, :], start=True,
                                           stop=True, skip_group_check=True)
                        mm.then_inc(s["v"], 1)
                        pe.wait_ge(s["vs"], i * (LV - 1) + v)
                        for c in range(CB):
                            pe.matmul(ps_w[c // 2][:, c % 2, 0, :], T[:, c, 1, :], V[:, c, 0, :], start=True, stop=True,
                                      skip_group_check=True)
                            mm = pe.matmul(ps_w[c // 2][:, c % 2, 1, :], T[:, c, 0, :], V[:, c, 1, :], start=True,
                                           stop=True, skip_group_check=True)
                        mm.then_inc(s["w"], 1)
                    pe.wait_ge(s["tt"], i * NTT + NTT)
                    for c in range(CB):
                        for q in range(2):
                            mm = pe.matmul(ps_v[c // 2][:, c % 2, q, :], Bm[:, c, q * P:(q + 1) * P], T[:, c, 1, :],
                                           start=True, stop=True, skip_group_check=True)
                    mm.then_inc(s["r"], 1)
                    pe.wait_ge(s["rs"], i + 1)
                    for c in range(CB):
                        pe.wait_ge(s["ms"], i * CB + c + 1)
                        for q in range(2):
                            mm = pe.matmul(ps_y[:, :], R[:, c, q, :], M[:, q, :], start=(q == 0), stop=(q == 1))
                        mm.then_inc(s["y"], 1)
                        pe.wait_ge(s["ys"], i * CB + c + 1)
                        for q in range(2):
                            mm = pe.matmul(ps_m[:, q, :], S[:, c, q * P:(q + 1) * P], Y[:, :], start=False, stop=True,
                                           skip_group_check=True)
                        mm.then_inc(s["m"], 1)

            @block.gpsimd
            def _(pool):
                pool.sem_inc(s["ms"], 1)


def apply_rotations(nc, K, M, MT, H):
    ps = nc.psum_tensor("ar_ps", [P, 2, D], F32)
    with ps as ps:
        with phase(nc, "ar", "turn cp") as (block, s):
            @block.tensor
            def _(pe):
                for q in range(2):
                    for k in range(2):
                        tr = pe.transpose(ps[:, k, q * P:(q + 1) * P], M[:, q, k * P:(k + 1) * P], K["ident"][:, :])
                tr.then_inc(s["turn"], 1)

            @block.vector
            def _(dve):
                dve.wait_ge(s["turn"], 1)
                dve.tensor_copy(MT[:, :, :], ps[:, :, :]).then_inc(s["cp"], 1)
        project(nc, "pr", K, K["X"], [(lambda k: MT[:, k, :], None, D, lambda t, u: H[:, bass.ds(t, 1), :], ACT.Copy)])


def program(nc, io, out, stop=99):
    with ExitStack() as ctx:
        ctx.enter_context(nc.allow_non_contiguous_dma(reason="small tables with a few numbers for each node or edge"))

        def sb(name, shape, dt=F32):
            return ctx.enter_context(nc.sbuf_tensor(name, shape, dt))

        def scratch(name, shape, dt=F32):
            return nc.dram_tensor(name, shape, dt, kind="Internal").ap()

        K = dict(
            gathers=[ctx.enter_context(nc.semaphore(f"gather{i}")) for i in range(2)],
            X=sb("X", [P, NT, D]), st=sb("st", [P, 4, NT]),
            ident=sb("ident", [P, P]), earlier=sb("earlier", [P, P]), ones=sb("ones", [P, P]), zero=sb("zero", [P, D + LO], BF16), later=sb("later", [P, P]),
            col=sb("col", [P, 1]), row=sb("row", [P, 2 * P]),
            raw_src=sb("raw_src", [P, RT], I32), raw_dst=sb("raw_dst", [P, RT], I32), raw_typ=sb("raw_typ", [P, RT], I32),
            raw_w=sb("raw_w", [P, RT]),
        )
        rows = lambda w: w.rearrange("(k p) n -> p k n", p=P)
        one = lambda v: v.rearrange("(a n) -> a n", a=1)
        flat = lambda v: v.rearrange("l n -> (l n)")
        wide = lambda v: v.partition_broadcast(P)
        dram = dict(x=io["x"], src=io["src"], dst=io["dst"], typ=io["typ"], w=io["w"])
        by = {}
        by["kloc_d"], by["oth_d"], by["tid_d"] = sb("kloc_d", [P, EX]), sb("oth_d", [P, EX], I32), sb("tid_d", [1, TX], I32)
        by["kloc_s"], by["oth_s"], by["tid_s"] = sb("kloc_s", [P, EX]), sb("oth_s", [P, EX], I32), sb("tid_s", [1, TX], I32)
        by["typ"] = sb("typ", [P, ET, TYPES])
        brk, last = sb("brk", [SBLK, 4, P]), sb("last", [P, ET])
        with ExitStack() as cs:
            for name, shape, dt in (
                    ("i_col", [P, 1], I32), ("i_row", [P, 2 * P], I32), ("i_tiles", [P, EX], I32), ("tiles", [P, EX], F32),
                    ("i_a", [P, 2], I32), ("i_b", [P, P], I32), ("pair_col", [P, 2], F32), ("pair_row", [P, P], F32),
                    ("odd_row", [P, P], F32), ("even_col", [P, 1], F32), ("same_pair", [P, P], F32),
                    ("before_pair", [P, P], F32), ("odd_prev", [P, P], F32), ("col1", [P, 1], F32)):
                K[name] = cs.enter_context(nc.sbuf_tensor(name, shape, dt))
            constants(nc, K, dram)
            for tag, key, other, kloc, oth, tid, typ in (
                    ("sd", K["raw_dst"], K["raw_src"], by["kloc_d"], by["oth_d"], by["tid_d"], None),
                    ("ss", K["raw_src"], K["raw_dst"], by["kloc_s"], by["oth_s"], by["tid_s"], by["typ"])):
                sort_edges(nc, K, tag, key, other, scratch(tag + "_keyrow", (RT, P), I32), scratch(tag + "_hirow", (RT, P), I32),
                           scratch(tag + "_rec", (ET * P, 4), I32), kloc, oth, tid, typ)
        segment_marks(nc, K, by["kloc_d"], brk, last)

        Hd, acc = sb("Hd", [P, NT, D]), sb("acc", [P, NT, D + HEADS2])
        H = Hd[:, :, :]
        tmp = acc[:, :, 0:D]

        with ExitStack() as c0:
            K["w0"] = c0.enter_context(nc.sbuf_tensor("w0", [P, 2, D + 1], F32))
            K["b0"] = c0.enter_context(nc.sbuf_tensor("b0", [1, D + 1], F32))
            K["att0"] = c0.enter_context(nc.sbuf_tensor("att0", [P, 2, D], F32))
            load(nc, "ld0", [
                (K["w0"][:, :, 0:D], rows(io["L0_WT"])), (K["w0"][:, :, D:D + 1], io["L0_mag_w"].rearrange("a (k p) -> p k a", p=P)),
                (K["b0"][:, 0:D], one(io["L0_b"])), (K["b0"][:, D:D + 1], one(io["L0_mag_b"])),
                (K["att0"][:, :, :].rearrange("p a d -> p (a d)"), wide(io["L0_attn_w"].rearrange("a n -> (a n)")))])
            maglog = c0.enter_context(nc.sbuf_tensor("maglog", [P, NT, 1], F32))
            p0 = c0.enter_context(nc.sbuf_tensor("p0", [P, NT, 1], F32))
            q0 = c0.enter_context(nc.sbuf_tensor("q0", [P, NT, 1], F32))
            peak = c0.enter_context(nc.sbuf_tensor("peak0", [P, NT, 1], F32))
            sall = c0.enter_context(nc.sbuf_tensor("sall0", [P, ET, 1], F32))
            fl = c0.enter_context(nc.sbuf_tensor("fl0", [P, ET, 2], F32))
            tmp0 = c0.enter_context(nc.sbuf_tensor("tmp0", [P, NT, D], F32))
            htab, ptab = scratch("htab0", (NP, D)), scratch("ptab0", (NP, 1))
            project(nc, "p0", K, K["X"], [
                (lambda k: K["w0"][:, k, 0:D], K["b0"][:, 0:D], D, lambda t, u: Hd[:, bass.ds(t, 1), :], ACT.Copy),
                (lambda k: K["w0"][:, k, D:D + 1], K["b0"][:, D:D + 1], 1, lambda t, u: maglog[:, bass.ds(t, 1), :], ACT.Copy)])
            layer0_nodes(nc, K, H, tmp0[:, :, :], maglog, p0, q0, htab, ptab)
            edge_scores(nc, "e0a", K, 1, by["kloc_d"], by["oth_d"], by["tid_d"], ptab, q0, sall)
            mask_scores(nc, "e0k", K, 1, by["kloc_d"], sall, None)
            segment_max(nc, "e0m", K, 1, by["kloc_d"], by["tid_d"], brk, last, sall, fl, peak)
            layer0_guard(nc, K, q0, peak)
            edge_sum(nc, "e0b", K, 1, by["kloc_d"], by["oth_d"], by["tid_d"], htab, peak, sall, acc)
            layer0_finish(nc, K, H, acc, tmp0[:, :, :])

        if stop > 1:
            with ExitStack() as c1:
                part = lambda name, shape: c1.enter_context(nc.sbuf_tensor(name, shape, F32))
                K["wqkv"], K["bqkv"] = part("wqkv", [P, 2, 3 * D]), part("bqkv", [1, 3 * D])
                K["wo1"], K["bo1"], K["eT"] = part("wo1", [P, 2, D]), part("bo1", [1, D]), part("eT", [P, 2, TYPES])
                K["ty"], K["lng"], K["lnb"] = part("ty", [TYPES, D]), part("lng", [P, D]), part("lnb", [P, D])
                Qb = c1.enter_context(nc.sbuf_tensor("Qb", [P, NT, D], F32))
                kvtab = scratch("kvtab", (NP, 2 * D))
                node = lambda buf: (lambda t, u: buf[:, bass.ds(t, 1), 0:D])
                dense(nc, "win", K, K["X"], io["Win"], io["b_in"], Hd, ACT.Copy)
                with nc.Fori(0, 3) as l:
                    of = lambda v: v[bass.ds(l, 1)].rearrange("a n -> (a n)")
                    load(nc, "ldl", [
                        (K["wqkv"][:, :, :], io["Wqkv"][bass.ds(l, 1)].rearrange("a (k p) n -> p (a k) n", p=P)),
                        (K["wo1"][:, :, :], io["Wo"][bass.ds(l, 1)].rearrange("a (k p) n -> p (a k) n", p=P)),
                        (K["eT"][:, :, :], io["eT"][bass.ds(l, 1)].rearrange("a (k p) n -> p (a k) n", p=P)),
                        (K["bqkv"][:, :], io["bqkv"][bass.ds(l, 1)]), (K["bo1"][:, :], io["bo"][bass.ds(l, 1)]),
                        (K["lng"][:, :], wide(of(io["ln_g"]))), (K["lnb"][:, :], wide(of(io["ln_b"])))])
                    type_rows(nc, K)
                    with nc.sbuf_tensor("kvst", [P, 5, 2 * D], F32) as kvst:
                        project(nc, "qkv", K, Hd, [
                            (lambda k: K["wqkv"][:, k, 0:D], K["bqkv"][:, 0:D], D, node(Qb), ACT.Copy),
                            (lambda k: K["wqkv"][:, k, D:3 * D], K["bqkv"][:, D:3 * D], 2 * D,
                             lambda t, u: kvst[:, u, :], ACT.Copy)],
                            store=lambda t, u: (kvtab[bass.ds(t * P, P), :], kvst[:, u, :]))
                    edge_attention(nc, "e1", K, by["kloc_s"], by["oth_s"], by["tid_s"], by["typ"], kvtab, Qb, acc)
                    project(nc, "wo", K, acc, [(lambda k: K["wo1"][:, k, :], None, D, node(Qb), ACT.Copy)],
                            extra=K["ty"][:, :])
                    layer1_update(nc, K, H, Qb[:, :, :])
                dense(nc, "mlp1", K, Hd, io["W1"], io["b1"], Qb, ACT.Relu)
                dense(nc, "mlp2", K, Qb, io["W2"], io["b2"], Hd, ACT.Copy)
                add_and_normalise(nc, "l1e", K, H, True, Qb[:, :, :])
        if stop > 2:
            with ExitStack() as c2:
                part = lambda name, shape: c2.enter_context(nc.sbuf_tensor(name, shape, F32))
                asrc, adst, selfs, peak, den = (part(n + "2", [P, NT, HEADS2]) for n in ("asrc", "adst", "selfs", "peak", "den"))
                sall = part("sall2", [P, ET, HEADS2])
                K["wg2"], K["att2"] = part("wg2", [P, 2, D]), part("att2", [P, 2, D])
                K["bias2"], K["gamma2"], K["beta2"] = (part(n, [P, D]) for n in ("bias2", "gamma2", "beta2"))
                load(nc, "ld2", [(K["wg2"][:, :, :], rows(io["L2_W"])), (K["bias2"][:, :], wide(io["L2_bias"])),
                                 (K["gamma2"][:, :], wide(io["L2_gamma"])), (K["beta2"][:, :], wide(io["L2_beta"])),
                                 (K["att2"][:, 0, :], wide(flat(io["att_src"]))), (K["att2"][:, 1, :], wide(flat(io["att_dst"])))])
                htab, ptab = scratch("htab2", (NP, D)), scratch("ptab2", (NP, HEADS2))
                project(nc, "wg2", K, K["X"], [(lambda k: K["wg2"][:, k, :], None, D, node(Hd), ACT.Copy)])
                layer2_nodes(nc, K, H, acc[:, :, 0:D], asrc, adst, selfs, htab, ptab)
                edge_scores(nc, "e2a", K, HEADS2, by["kloc_d"], by["oth_d"], by["tid_d"], ptab, adst, sall)
                mask_scores(nc, "e2k", K, HEADS2, by["kloc_d"], sall, 0.2)
                with nc.sbuf_tensor("fl2", [P, ET, HEADS2 + 1], F32) as fl:
                    segment_max(nc, "e2m", K, HEADS2, by["kloc_d"], by["tid_d"], brk, last, sall, fl, peak)
                layer2_self(nc, K, selfs, peak)
                edge_sum(nc, "e2b", K, HEADS2, by["kloc_d"], by["oth_d"], by["tid_d"], htab, peak, sall, acc)
                with nc.sbuf_tensor("tmp2", [P, NT, D], F32) as tmp2:
                    layer2_finish(nc, K, H, acc, tmp2[:, :, :], selfs, den)

        if stop > 3:
            with ExitStack() as c3:
                part = lambda name, shape, dt=F32: c3.enter_context(nc.sbuf_tensor(name, shape, dt))
                M, MT, batches = part("M", [P, 2, D]), part("MT", [P, 2, D]), part("batches", [1, 1], I32)
                steps = scratch("steps", (RT * P, 4))
                rotation_steps(nc, K, steps, batches)
                rotation_matrix(nc, K, steps, batches, M)
                apply_rotations(nc, K, M, MT, Hd)
                add_and_normalise(nc, "l3e", K, H, False, acc[:, :, 0:D])

        with phase(nc, "out", "st") as (block, s):
            @block.sync
            def _(sp):
                sp.dma_start(out[0:(NT - 1) * P, :].rearrange("(t p) d -> p t d", p=P),
                             K["X"][:, 0:NT - 1, :]).then_inc(s["st"], 16)
                sp.dma_start(out[(NT - 1) * P:N, :], K["X"][0:LASTN, NT - 1, :]).then_inc(s["st"], 16)
                sp.wait_ge(s["st"], 32)


def mask_scores(nc, tag, K, H, kloc, sall, slope):
    with ExitStack() as ctx:
        pad = ctx.enter_context(nc.sbuf_tensor(f"{tag}_pad", [P, ET], F32))
        with phase(nc, tag, "chain") as (block, s):
            @block.vector
            def _(dve):
                link = linker(dve, s["chain"])
                if slope is not None:
                    link(dve.scalar_tensor_tensor(out=sall[:, :, :], in0=sall[:, :, :], scalar=slope,
                                                  in1=sall[:, :, :], op0=ALU.mult, op1=ALU.max))
                link(dve.tensor_scalar(pad[:, :], kloc[:, 0:ET], 0.0, -BIG, ALU.is_lt, ALU.mult))
                link(dve.tensor_tensor(sall[:, :, :], sall[:, :, :], pad[:, :].unsqueeze(2).broadcast_to([P, ET, H]),
                                       ALU.add))


def kernel(**inputs):
    import numpy as _np
    import concourse.bacc as _bacc
    from concourse import mybir as _mybir
    from concourse.bass_utils import run_bass_kernel_spmd as _run

    laid = {"x": inputs["x"], "src": inputs["src"], "dst": inputs["dst"], "typ": inputs["edge_type_3"],
            "w": inputs["edge_weight"], "L0_WT": inputs["L0_gnn_W"].T, "L0_b": inputs["L0_gnn_b"],
            "L0_mag_w": inputs["L0_gnn_mag_w"], "L0_mag_b": inputs["L0_gnn_mag_b"], "L0_attn_w": inputs["L0_gnn_attn_w"],
            "Win": inputs["L1_gnn_Win"].T, "W1": inputs["L1_gnn_W1"].T, "W2": inputs["L1_gnn_W2"].T,
            "b_in": inputs["L1_gnn_b_in"], "b1": inputs["L1_gnn_b1"], "b2": inputs["L1_gnn_b2"],
            "eT": inputs["L1_gnn_Eemb"].transpose(0, 2, 1), "ln_g": inputs["L1_gnn_ln_g"], "ln_b": inputs["L1_gnn_ln_b"],
            "L2_W": inputs["L2_gnn_W"], "L2_bias": inputs["L2_gnn_bias"], "L2_gamma": inputs["L2_gnn_gamma"],
            "L2_beta": inputs["L2_gnn_beta"], "att_src": inputs["L2_gnn_att_src"], "att_dst": inputs["L2_gnn_att_dst"]}
    laid["Wqkv"] = _np.concatenate([_np.asarray(inputs["L1_gnn_W" + c]).transpose(0, 2, 1) for c in "qkv"], axis=2)
    laid["bqkv"] = _np.concatenate([_np.asarray(inputs["L1_gnn_b" + c]) for c in "qkv"], axis=1)
    laid["Wo"], laid["bo"] = inputs["L1_gnn_Wo"].transpose(0, 2, 1), inputs["L1_gnn_bo"]
    nc = _bacc.Bacc("TRN2", target_bir_lowering=False, num_devices=1)
    arrays, io = {}, {}
    for name, a in laid.items():
        a = _np.ascontiguousarray(a)
        arrays[f"in_{name}_dram"] = a
        io[name] = nc.dram_tensor(f"in_{name}_dram", a.shape, _mybir.dt.from_np(a.dtype), kind="ExternalInput").ap()
    out = nc.dram_tensor("out_0_dram", (N, D), F32, kind="ExternalOutput").ap()
    program(nc, io, out)
    r = _run(nc, [arrays], core_ids=[0])
    return r.results[0]["out_0_dram"]
```
